# Optimizing a Trainium2 kernel written in Bass

```python
import numpy as np
import jax
import jax.numpy as jnp

def _softmax(x, axis=-1):
    return jax.nn.softmax(x, axis=axis)

def _gelu(x):
    return jax.nn.gelu(x, approximate=True)

def _silu(x):
    return jax.nn.silu(x)

def _sigmoid(x):
    return jax.nn.sigmoid(x)

def _layernorm(x, axis=-1, eps=1e-05):
    m = jnp.mean(x, axis=axis, keepdims=True)
    v = jnp.var(x, axis=axis, keepdims=True)
    return (x - m) / jnp.sqrt(v + eps)

def _scatter_add(tgt, idx, src, axis=0):
    return tgt.at[idx].add(src)

def _segment_sum(src, seg, n):
    return jax.ops.segment_sum(src, seg, n)
kernel_name = 'mk_decoder_preln_d1_seqx_r2_550fe2'

def setup_inputs(seed: int=0):
    np.random.seed(seed)
    _w = jnp.asarray

    def _rec_inputs():
        import jax
        import jax.numpy as jnp
        _rk = jax.random.key(seed)
        x = -0.0002928 + 1 * jax.random.normal(jax.random.fold_in(_rk, 1), (16, 224, 512), jnp.float32)
        _lenS = 224 - jax.random.randint(jax.random.fold_in(_rk, 7), (16,), 0, max(1, 224 // 4) + 1, jnp.int32)
        _lenS2 = 750 - jax.random.randint(jax.random.fold_in(_rk, 8), (16,), 0, max(1, 750 // 4) + 1, jnp.int32)
        _ctx_512P = jax.random.normal(jax.random.fold_in(_rk, 11), (16, 16, 256), jnp.float32)
        _ctx_512c = jax.random.dirichlet(jax.random.fold_in(_rk, 511), 0.3 * jnp.ones((16,), jnp.float32), (16, 750))
        _ctx_512t = jnp.einsum('bsk,bkd->bsd', _ctx_512c, _ctx_512P)
        _ctx_512t = _ctx_512t * jax.lax.rsqrt(jnp.mean(jnp.square(_ctx_512t)) + 1e-12) * 0.953939
        ctx_512 = -0.000514642 + 1.00011 * (_ctx_512t + 0.3 * jax.random.normal(jax.random.fold_in(_rk, 611), (16, 750, 256), jnp.float32))
        return (x, ctx_512)
    x, ctx_512 = _rec_inputs()

    def _L0_attn_setup():
        import jax, jax.numpy as jnp
        import numpy as np
        D_MODEL = 512
        RANK = 128
        INIT_ALPHA = 0.5
        key = jax.random.key(seed)
        ks = jax.random.split(key, 12)
        D, R = (D_MODEL, RANK)
        s = 0.02
        return {'x': jax.random.normal(ks[0], (4, 1024, D), dtype=jnp.float32), 'Wq': jax.random.normal(ks[1], (D, D), dtype=jnp.float32) * s, 'Wk': jax.random.normal(ks[2], (D, D), dtype=jnp.float32) * s, 'Wo': jax.random.normal(ks[3], (D, D), dtype=jnp.float32) * s, 'U_b': jax.random.normal(ks[4], (D, R), dtype=jnp.float32) * s, 'V_b': jax.random.normal(ks[5], (D, R), dtype=jnp.float32) * s, 'W_b': jax.random.normal(ks[6], (D, R), dtype=jnp.float32) * s, 'bias_b': jnp.zeros((D,), dtype=jnp.float32), 'U_t': jax.random.normal(ks[7], (D, R), dtype=jnp.float32) * s, 'V_t': jax.random.normal(ks[8], (D, R), dtype=jnp.float32) * s, 'W_t': jax.random.normal(ks[9], (D, R), dtype=jnp.float32) * s, 'X_t': jax.random.normal(ks[10], (D, R), dtype=jnp.float32) * s, 'bias_t': jnp.zeros((D,), dtype=jnp.float32), 'alpha': jnp.asarray(INIT_ALPHA, dtype=jnp.float32)}
    _L0_attn_all = _L0_attn_setup()
    _L0_attn_in = {k: v for k, v in _L0_attn_all.items() if k in ('Wq', 'Wk', 'Wo', 'U_b', 'V_b', 'W_b', 'bias_b', 'U_t', 'V_t', 'W_t', 'X_t', 'bias_t', 'alpha')}
    del _L0_attn_all

    def _L0_xattn_setup():
        import jax, jax.numpy as jnp
        import numpy as np
        DIM = 512
        LATENT_DIM = 256
        NUM_HEADS = 16
        HEAD_DIM = DIM // NUM_HEADS
        SCALE = HEAD_DIM ** (-0.5)
        key = jax.random.key(seed)
        k1, k2, k3, k4, k5 = jax.random.split(key, 5)
        B, xN, zN = (2, 1024, 1024)
        x = jax.random.normal(k1, (B, xN, DIM), dtype=jnp.float32)
        z = jax.random.normal(k2, (B, zN, LATENT_DIM), dtype=jnp.float32)
        Wq = jax.random.normal(k3, (DIM, DIM), dtype=jnp.float32) * DIM ** (-0.5)
        Wkv = jax.random.normal(k4, (2 * DIM, LATENT_DIM), dtype=jnp.float32) * LATENT_DIM ** (-0.5)
        Wo = jax.random.normal(k5, (DIM, DIM), dtype=jnp.float32) * DIM ** (-0.5)
        return {'x': x, 'z': z, 'Wq': Wq, 'Wkv': Wkv, 'Wo': Wo}
    _L0_xattn_all = _L0_xattn_setup()
    _L0_xattn_in = {k: v for k, v in _L0_xattn_all.items() if k in ('Wq', 'Wkv', 'Wo')}
    del _L0_xattn_all

    def _L0_ffn_setup():
        import jax, jax.numpy as jnp
        import numpy as np
        B, S, D, E, H, K = (64, 1024, 512, 32, 2048, 8)
        key = jax.random.key(seed)
        k0, k1, k2, k3 = jax.random.split(key, 4)
        x = jax.random.normal(k0, (B, S, D), jnp.float32)
        gate_w = jax.random.normal(k1, (E, D), jnp.float32) * (1.0 / np.sqrt(D))
        gate_b = jnp.zeros((E,), jnp.float32)
        w1 = jax.random.normal(k2, (E, D + 1, H), jnp.float32) * (1.0 / np.sqrt(D + 1))
        w2 = jax.random.normal(k3, (E, H + 1, D), jnp.float32) * (1.0 / np.sqrt(H + 1))
        return {'x': x, 'gate_w': gate_w, 'gate_b': gate_b, 'w1': w1, 'w2': w2}
    _L0_ffn_all = _L0_ffn_setup()
    _L0_ffn_in = {k: v for k, v in _L0_ffn_all.items() if k in ('gate_w', 'gate_b', 'w1', 'w2')}
    del _L0_ffn_all
    return {'x': x, 'ctx_512': ctx_512, 'L0_attn_Wq': _L0_attn_in['Wq'], 'L0_attn_Wk': _L0_attn_in['Wk'], 'L0_attn_Wo': _L0_attn_in['Wo'], 'L0_attn_U_b': _L0_attn_in['U_b'], 'L0_attn_V_b': _L0_attn_in['V_b'], 'L0_attn_W_b': _L0_attn_in['W_b'], 'L0_attn_bias_b': _L0_attn_in['bias_b'], 'L0_attn_U_t': _L0_attn_in['U_t'], 'L0_attn_V_t': _L0_attn_in['V_t'], 'L0_attn_W_t': _L0_attn_in['W_t'], 'L0_attn_X_t': _L0_attn_in['X_t'], 'L0_attn_bias_t': _L0_attn_in['bias_t'], 'L0_attn_alpha': _L0_attn_in['alpha'], 'L0_xattn_Wq': _L0_xattn_in['Wq'], 'L0_xattn_Wkv': _L0_xattn_in['Wkv'], 'L0_xattn_Wo': _L0_xattn_in['Wo'], 'L0_ffn_gate_w': _L0_ffn_in['gate_w'], 'L0_ffn_gate_b': _L0_ffn_in['gate_b'], 'L0_ffn_w1': _L0_ffn_in['w1'], 'L0_ffn_w2': _L0_ffn_in['w2']}

def reference(x, ctx_512, L0_attn_Wq, L0_attn_Wk, L0_attn_Wo, L0_attn_U_b, L0_attn_V_b, L0_attn_W_b, L0_attn_bias_b, L0_attn_U_t, L0_attn_V_t, L0_attn_W_t, L0_attn_X_t, L0_attn_bias_t, L0_attn_alpha, L0_xattn_Wq, L0_xattn_Wkv, L0_xattn_Wo, L0_ffn_gate_w, L0_ffn_gate_b, L0_ffn_w1, L0_ffn_w2):
    import jax
    import jax.numpy as jnp

    def _L0_attn_ref(x, Wq, Wk, Wo, U_b, V_b, W_b, bias_b, U_t, V_t, W_t, X_t, bias_t, alpha):
        import jax, jax.numpy as jnp
        import numpy as np
        D_MODEL = 512
        RANK = 128
        INIT_ALPHA = 0.5
        B, T, D = x.shape
        Q = x @ Wq.T
        K = x @ Wk.T
        counts = jnp.arange(1, T + 1, dtype=x.dtype)[None, :, None]
        Z = jnp.cumsum(x, axis=1) / counts
        a_b = Q @ V_b
        c_b = jnp.cumsum(K @ W_b, axis=1)
        bil = a_b * c_b @ U_b.T
        a_t = Q @ V_t
        c_t = jnp.cumsum(K @ W_t, axis=1)
        z_t = Z @ X_t
        tri = a_t * z_t * c_t @ U_t.T
        out = (bil + alpha * tri) / counts + (bias_b + alpha * bias_t)
        return out @ Wo.T

    def _L0_xattn_ref(x, z, Wq, Wkv, Wo):
        import jax, jax.numpy as jnp
        import numpy as np
        DIM = 512
        LATENT_DIM = 256
        NUM_HEADS = 16
        HEAD_DIM = DIM // NUM_HEADS
        SCALE = HEAD_DIM ** (-0.5)
        B, xN, _ = x.shape
        _, zN, _ = z.shape
        Q = (x @ Wq.T).reshape(B, xN, NUM_HEADS, HEAD_DIM)
        KV = (z @ Wkv.T).reshape(B, zN, 2, NUM_HEADS, HEAD_DIM)
        K = KV[:, :, 0]
        V = KV[:, :, 1]
        attn = jnp.einsum('bqhd,bkhd->bhqk', Q, K) * SCALE
        attn = jax.nn.softmax(attn, axis=-1)
        O = jnp.einsum('bhqk,bkhd->bqhd', attn, V).reshape(B, xN, DIM)
        return O @ Wo.T

    def _L0_ffn_ref(x, gate_w, gate_b, w1, w2):
        import jax, jax.numpy as jnp
        import numpy as np
        B, S, D, E, H, K = (64, 1024, 512, 32, 2048, 8)
        b, s, d = x.shape
        logits = jnp.einsum('bsd,ed->bse', x, gate_w) + gate_b
        probs = jax.nn.softmax(logits, axis=-2)
        vals_t, idx_t = jax.lax.top_k(probs.transpose(0, 2, 1), K)
        vals = vals_t.transpose(0, 2, 1)
        idx = idx_t.transpose(0, 2, 1)
        flat_idx = idx.reshape(b, K * E)
        tok = jnp.take_along_axis(x, flat_idx[:, :, None], axis=1)
        tok = tok.reshape(b, K, E, d)
        merged = jnp.einsum('bked,bke->bed', tok, vals)
        ones = jnp.ones(merged.shape[:-1] + (1,), merged.dtype)
        h = jnp.einsum('bei,eih->beh', jnp.concatenate([merged, ones], -1), w1)
        h = jax.nn.gelu(h, approximate=False)
        o = jnp.einsum('bej,ejo->beo', jnp.concatenate([h, ones], -1), w2)
        out_tok = jnp.einsum('beo,bke->bkeo', o, vals).reshape(b, K * E, d)
        out = jnp.zeros_like(x).at[jnp.arange(b)[:, None], flat_idx].add(out_tok)
        return out
    x = x + _L0_attn_ref(_layernorm(x, axis=-1), L0_attn_Wq, L0_attn_Wk, L0_attn_Wo, L0_attn_U_b, L0_attn_V_b, L0_attn_W_b, L0_attn_bias_b, L0_attn_U_t, L0_attn_V_t, L0_attn_W_t, L0_attn_X_t, L0_attn_bias_t, L0_attn_alpha)
    x = x + _L0_xattn_ref(_layernorm(x, axis=-1), ctx_512, L0_xattn_Wq, L0_xattn_Wkv, L0_xattn_Wo)
    x = x + _L0_ffn_ref(_layernorm(x, axis=-1), L0_ffn_gate_w, L0_ffn_gate_b, L0_ffn_w1, L0_ffn_w2)
    return x

_drawn_inputs = setup_inputs


def setup_inputs(seed=0):
    import zlib

    import numpy as np

    out = dict(_drawn_inputs(seed))
    spreads = {'L0_attn_bias_b': (0.0, 0.8), 'L0_attn_bias_t': (0.0, 2.0), 'L0_ffn_gate_b': (0.0, 0.8)}
    factors = {'L0_attn_Wq': 8.0,
     'L0_attn_Wk': 8.0,
     'L0_attn_U_b': 8.0,
     'L0_attn_V_b': 8.0,
     'L0_attn_W_b': 8.0,
     'L0_attn_U_t': 8.0,
     'L0_attn_V_t': 8.0,
     'L0_attn_W_t': 8.0,
     'L0_attn_X_t': 8.0,
     'ctx_512': 4.086,
     'L0_xattn_Wq': 8.0,
     'L0_xattn_Wkv': 3.671,
     'L0_xattn_Wo': 3.692,
     'L0_ffn_gate_w': 8.0,
     'L0_ffn_w1': 8.0,
     'L0_ffn_w2': 8.0}
    for name, (base, spread) in spreads.items():
        noise = np.random.default_rng([zlib.crc32(name.encode()), seed]).standard_normal(out[name].shape)
        drawn = base * np.exp(spread * noise) if base else spread * noise
        out[name] = jnp.asarray(drawn.astype(out[name].dtype))
    for name, factor in factors.items():
        out[name] = (out[name] * factor).astype(out[name].dtype)
    return out
```

```python
from contextlib import ExitStack

import concourse.bass as bass
from concourse import mybir

F32 = mybir.dt.float32
F32R = mybir.dt.float32r
ALU = mybir.AluOpType
ACT = mybir.ActivationFunctionType
AX = mybir.AxisListType

P = 128
BANK = 512
TOPK = 8
EPS = 1e-5
NEG = -3.0e38

TIMETABLE = (
    [(0, s, j) for s, j in ((0, "q2"), (1, "k2.0"), (2, "k2.1"), (4, "v4"), (6, "v5"),
                            (9, "xt0"), (10, "xt1"), (12, "out0"), (13, "pa"), (14, "out1"))]
    + [(1, s, j) for s, j in ((0, "q3"), (1, "k3.0"), (2, "k3.1"), (3, "pc"), (4, "pz"),
                              (5, "ct0"), (6, "ct1"), (7, "ct2"), (8, "ct3"), (9, "mix0"),
                              (10, "mix1"))]
    + [(2, s, j) for s, j in ((1, "yt0"), (2, "yt1"), (3, "q0"), (4, "k0.0"), (5, "k0.1"),
                              (6, "rt0"), (7, "rt1"), (9, "gate"), (12, "wt0"), (13, "wt1"),
                              (15, "merge"))]
    + [(3, s, j) for s, j in ((0, "mt"), (1, "q1"), (2, "k1.0"), (3, "k1.1"), (7, "v0"),
                              (8, "v1"), (11, "v2"), (12, "v3"))]
)
NEXT = {"xt0", "xt1", "pa", "pc", "pz", "mix0", "mix1", "yt0", "yt1", "ct0", "ct1", "ct2", "ct3",
        "q0", "k0.0", "k0.1", "q1", "k1.0", "k1.1", "v0", "v1", "v2", "v3"}
PAST = {"out0", "out1", "rt0", "rt1", "gate", "wt0", "wt1", "merge", "mt"}
ORDER = [j for _, _, j in TIMETABLE]
STEPS = 16
UNIT_AT = 1
PV_AT = {6: 0, 10: 1}
LAST_PV_AT = 1
SUM_AT = {6: 0, 10: 1, 14: 2}
TURN_AT = 11
ROWS_AT = 13
LATE_AT = 2


COST = {"q": 9, "k": 8, "v": 10, "x": 3, "y": 3, "r": 3, "o": 20, "c": 3, "p": 12, "m": 8, "g": 9,
        "w": 1}


def maxima_at(kt, s):
    def weight(i):
        if i == LATE_AT + 1:
            return 0
        return 3 + sum(min(COST[j[0]], 9) for g, st, j in TIMETABLE if (g, st) == (kt, i))
    if s >= TURN_AT:
        return range(0)
    total = sum(weight(i) for i in range(TURN_AT))
    upto = [round(16 * sum(weight(i) for i in range(n)) / total) for n in (s, s + 1)]
    return range(*upto)


def build(nc, x, ctx_in, aWq, aWk, aWo, U_b, V_b, W_b, bias_b, U_t, V_t, W_t, X_t, bias_t, alpha,
          xWq, xWkv, xWo, gate_w, gate_b, w1, w2, out):
    B, T, D = x.shape
    _, S, DC = ctx_in.shape
    R = V_b.shape[1]
    E, _, H = w1.shape
    NH = 16
    HD = D // NH
    SCALE = float(HD) ** -0.5
    KD, KC = D // P, DC // P
    TT = T // 2
    SK = 125
    NK = S // SK
    SC = (0, 376, S)
    G = KD
    LAST = B - 1
    assert T == 224 and NK * SK == S and R == P and G == 4 and 4 * HD == P and E == 32

    PRO = ([j for j in ("xt0", "xt1", "pa", "pc", "pz", "mix0", "mix1", "yt0", "yt1")]
           + [j for j in ORDER if j[:2] == "ct"] + ["q0", "k0.0", "k0.1", "q1", "k1.0", "k1.1",
              "v0", "v1", "v2", "v3"])
    SEQ = {"pro": PRO, "first": [j for j in ORDER if j not in PAST], "mid": ORDER,
           "last": [j for j in ORDER if j not in NEXT], "tail": [j for j in ORDER if j in PAST]}
    N_PRO, N_FIRST, N_MID = len(PRO), len(SEQ["first"]), len(ORDER)
    BASE = {"pro": 0, "first": N_PRO, "mid": N_PRO + N_FIRST - N_MID,
            "last": N_PRO + N_FIRST - N_MID + N_MID * LAST}
    BASE["tail"] = BASE["last"] + len(SEQ["last"])
    assert N_MID % 2 == 0

    def place(job, kind):
        return BASE[kind] + SEQ[kind].index(job)

    def number(job, kind, b):
        n = place(job, kind)
        return b * N_MID + n if kind == "mid" else n

    def batch_of(job, kind, b):
        return b + 1 if job in NEXT else b - 1 if job in PAST else b

    def before(job, kind, b):
        n = SEQ[kind].index(job)
        if n >= 2:
            p = SEQ[kind][n - 2]
            return p, batch_of(p, kind, b)
        if kind == "pro":
            return None
        if kind == "tail":
            p = SEQ["last"][n - 2]
            return p, batch_of(p, "last", b - 1)
        return PRO[n - 2], b

    es = ExitStack()
    with es:
        def sem(name):
            return es.enter_context(nc.semaphore(name))

        def sb(stack, name, shape, dt=F32):
            return stack.enter_context(nc.sbuf_tensor(name, shape, dt))

        bank = [es.enter_context(nc.psum_tensor(f"bank{i}", [P, BANK], F32)) for i in range(8)]
        router = nc.dram_tensor("router", [B, E, T], F32).ap()
        o_parts = nc.dram_tensor("o_parts", [B, 4, E, D], F32).ap()

        ident = sb(es, "ident", [P, P])
        merged_T = sb(es, "merged_T", [P, KD, E, B])

        lay = ExitStack()
        ones = sb(lay, "ones", [P, T])
        inv_count = sb(lay, "inv_count", [P, T])
        halves = sb(lay, "halves", [P, 2])
        eps_tile = sb(lay, "eps_tile", [P, 2])
        relay = sb(lay, "relay", [1, 8])
        in_q = sb(lay, "in_q", [P, KD, 2 * R])
        in_k = sb(lay, "in_k", [P, KD, 2 * R])
        in_z = sb(lay, "in_z", [P, KD, R])
        mix_out = sb(lay, "mix_out", [P, 2, D])
        bias_row = sb(lay, "bias_row", [TT, D])
        wq_T = sb(lay, "wq_T", [P, KD, D])
        wk_T = sb(lay, "wk_T", [P, KC, D])
        wv_T = sb(lay, "wv_T", [P, KC, D])
        wo_T = sb(lay, "wo_T", [P, KD, D])
        gate_T = sb(lay, "gate_T", [P, KD, E])
        gate_bias = sb(lay, "gate_bias", [E, 1])

        with ExitStack() as st:
            n_aq = sb(st, "n_aq", [P, KD, D])
            n_ak = sb(st, "n_ak", [P, KD, D])
            n_ao = sb(st, "n_ao", [P, KD, D])
            n_xq = sb(st, "n_xq", [P, KD, D])
            n_xo = sb(st, "n_xo", [P, KD, D])
            n_kv = sb(st, "n_kv", [P, 2 * KD, DC])
            vv = sb(st, "vv", [P, KD, 2 * R])
            ww = sb(st, "ww", [P, KD, 2 * R])
            uu = sb(st, "uu", [P, 2, KD, R])
            ao_T = sb(st, "ao_T", [P, KD, D])
            n_gate = sb(st, "n_gate", [E, D])
            bcol = sb(st, "bcol", [P, 2, KD])
            bmix = sb(st, "bmix", [P, KD])
            bwide = sb(st, "bwide", [P, KD, TT])
            al = sb(st, "al", [P, 1])
            s_load = sem("s_load")
            s_mv = sem("s_mv")
            s_iz = sem("s_iz")
            s_id = sem("s_id")
            s_full = sem("s_full")
            s_out = sem("s_out")
            s_one = sem("s_one")
            s_cnt = sem("s_cnt")
            s_bias = sem("s_bias")

            rows = lambda w: w.rearrange("(k p) n -> p k n", p=P)
            loads = [(n_xq[:], rows(xWq)), (n_ao[:], rows(aWo)), (n_xo[:], rows(xWo)),
                     (n_kv[:], rows(xWkv)), (n_gate[:], gate_w), (n_aq[:], rows(aWq)),
                     (vv[:, :, 0:R], rows(V_b)), (vv[:, :, R:2 * R], rows(V_t)),
                     (n_ak[:], rows(aWk)), (ww[:, :, 0:R], rows(W_b)),
                     (ww[:, :, R:2 * R], rows(W_t)), (uu[:, 0], rows(U_b)), (uu[:, 1], rows(U_t)),
                     (in_z[:], rows(X_t)), (gate_bias[:], gate_b.rearrange("(p o) -> p o", o=1)),
                     (bcol[:, 0, :], bias_b.rearrange("(k p) -> p k", p=P)),
                     (bcol[:, 1, :], bias_t.rearrange("(k p) -> p k", p=P)),
                     (al[:], alpha.to_broadcast((P, 1)))]

            flips = []
            for src, dst, kin in ((n_xq, wq_T, KD), (n_ao, ao_T, KD), (n_xo, wo_T, KD)):
                for i in range(kin):
                    flips.append([(src[:, o, i * P:(i + 1) * P], dst[:, i, :]) for o in range(KD)])
            for h, dst in ((0, wk_T), (1, wv_T)):
                for i in range(KC):
                    flips.append([(n_kv[:, h * KD + o, i * P:(i + 1) * P], dst[:, i, :])
                                  for o in range(KD)])
            NF = len(flips)
            N_SETUP = NF + 1 + 2 * KD + 2 + 1

            with nc.Block() as block:
                @block.sync
                def _(sp):
                    for dst, src in loads:
                        with nc.allow_non_contiguous_dma("bias columns"):
                            sp.dma_start(dst, src).then_inc(s_load, 16)

                @block.gpsimd
                def _(pool):
                    nc.gpsimd.memset(ident[:], 0.0).then_inc(s_iz, 1)
                    pool.wait_ge(s_iz, 1)
                    nc.gpsimd.affine_select(out=ident[:], in_=ident[:], compare_op=ALU.not_equal,
                                            fill=1.0, base=0, pattern=[[-1, P]],
                                            channel_multiplier=1).then_inc(s_id, 1)
                    nc.gpsimd.memset(halves[:], -0.5)
                    nc.gpsimd.memset(eps_tile[:], EPS)
                    nc.gpsimd.memset(relay[:], 0.0)

                @block.tensor
                def _(pe):
                    pe.wait_ge(s_id, 1)
                    pe.wait_ge(s_load, 16 * len(loads))
                    n = 0
                    for group in flips:
                        if n >= 8:
                            pe.wait_ge(s_out, n - 7)
                        for o, (src, _) in enumerate(group):
                            last = nc.tensor.transpose(bank[n % 8][:, o * P:(o + 1) * P], src,
                                                       ident[:])
                        last.then_inc(s_full, 1)
                        n += 1
                    pe.wait_ge(s_out, n - 7)
                    for kd in range(KD):
                        last = nc.tensor.transpose(bank[n % 8][:, kd * E:(kd + 1) * E],
                                                   n_gate[:, kd * P:(kd + 1) * P],
                                                   ident[0:E, 0:E])
                    last.then_inc(s_full, 1)
                    n += 1
                    for w, v in ((n_aq, vv), (n_ak, ww)):
                        for m in range(KD):
                            pe.wait_ge(s_out, n - 7)
                            for k in range(KD):
                                last = nc.tensor.matmul(bank[n % 8][:, 0:2 * R],
                                                        w[:, k, m * P:(m + 1) * P], v[:, k, :],
                                                        start=(k == 0), stop=(k == KD - 1))
                            last.then_inc(s_full, 1)
                            n += 1
                    for g in range(2):
                        pe.wait_ge(s_out, n - 7)
                        for k in range(KD):
                            last = nc.tensor.matmul(bank[n % 8][:], uu[:, g, k, :], ao_T[:, k, :],
                                                    start=(k == 0), stop=(k == KD - 1))
                        last.then_inc(s_full, 1)
                        n += 1
                    pe.wait_ge(s_out, n - 7)
                    pe.wait_ge(s_bias, 3)
                    for k in range(KD):
                        last = nc.tensor.matmul(bank[n % 8][0:TT, :], bwide[:, k, :], ao_T[:, k, :],
                                                start=(k == 0), stop=(k == KD - 1))
                    last.then_inc(s_full, 1)
                    assert n + 1 == N_SETUP

                @block.scalar
                def _(act):
                    n = 0
                    for group in flips:
                        act.wait_ge(s_full, n + 1)
                        nc.scalar.copy(group[0][1], bank[n % 8][:]).then_inc(s_out, 1)
                        n += 1
                    act.wait_ge(s_full, n + 1)
                    nc.scalar.copy(gate_T[:].rearrange("p k e -> p (k e)"),
                                   bank[n % 8][:, 0:KD * E]).then_inc(s_out, 1)
                    n += 1
                    for dst in (in_q, in_k):
                        for m in range(KD):
                            act.wait_ge(s_full, n + 1)
                            nc.scalar.copy(dst[:, m, :], bank[n % 8][:, 0:2 * R]).then_inc(s_out, 1)
                            n += 1
                    act.wait_ge(s_full, n + 1)
                    nc.scalar.copy(mix_out[:, 0, :], bank[n % 8][:]).then_inc(s_out, 1)
                    n += 1
                    act.wait_ge(s_full, n + 1)
                    nc.scalar.mul(mix_out[:, 1, :], bank[n % 8][:], al[:, 0:1]).then_inc(s_out, 1)
                    n += 1
                    act.wait_ge(s_full, n + 1)
                    nc.scalar.copy(bias_row[:], bank[n % 8][0:TT, :]).then_inc(s_out, 1)

                @block.vector
                def _(dve):
                    nc.vector.memset(ones[:], 1.0).then_inc(s_one, 1)
                    dve.wait_ge(s_one, 1)
                    nc.vector.tensor_tensor_scan(inv_count[:], ones[:], ones[:], 0.0, ALU.mult,
                                                 ALU.add).then_inc(s_cnt, 1)
                    dve.wait_ge(s_cnt, 1)
                    nc.vector.reciprocal(inv_count[:], inv_count[:]).then_inc(s_cnt, 1)
                    dve.wait_ge(s_load, 16 * len(loads))
                    nc.vector.tensor_scalar(bmix[:], bcol[:, 1, :], al[:, 0:1], None,
                                            ALU.mult).then_inc(s_bias, 1)
                    dve.wait_ge(s_bias, 1)
                    nc.vector.tensor_tensor(bmix[:], bmix[:], bcol[:, 0, :],
                                            ALU.add).then_inc(s_bias, 1)
                    dve.wait_ge(s_bias, 2)
                    nc.vector.tensor_copy(bwide[:], bmix[:].unsqueeze(2).to_broadcast([P, KD, TT])
                                          ).then_inc(s_bias, 1)

        x_in = sb(lay, "x_in", [TT, 2, D])
        x1 = sb(lay, "x1", [TT, 2, D])
        x1_kept = sb(lay, "x1_kept", [TT, 2, D])
        x2 = sb(lay, "x2", [TT, 2, D])
        xh = sb(lay, "xh", [TT, 2, D])
        xr = sb(lay, "xr", [TT, 2, D])
        stats = sb(lay, "stats", [TT, 3, 2, 6])
        mean_var = sb(lay, "mean_var", [TT, 3, 2, 2])
        rstd = sb(lay, "rstd", [TT, 3, 2])
        ctx_nat = sb(lay, "ctx_nat", [SK, NK, DC])
        ctx_T = sb(lay, "ctx_T", [P, KC, S])
        xT = sb(lay, "xT", [P, KD, T])
        yT = sb(lay, "yT", [P, KD, T])
        rT = xT
        a_mix = sb(lay, "a_mix", [P, 2, T])
        c_mix = sb(lay, "c_mix", [P, 2, T])
        z_mix = sb(lay, "z_mix", [P, T])
        g_mix = a_mix
        k_hi = sb(lay, "k_hi", [P, S], F32R)
        k_lo = sb(lay, "k_lo", [P, S], F32R)
        q_hi = sb(lay, "q_hi", [P, T], F32R)
        q_lo = sb(lay, "q_lo", [P, T], F32R)
        k_st = [sb(lay, f"k_st{i}", [3 * HD + 2, 4, S], F32R) for i in range(G)]
        q_st = [sb(lay, f"q_st{i}", [3 * HD + 2, 4, T], F32R) for i in range(G)]
        maxes = sb(lay, "maxes", [TT, 4, 2, 2])
        q_max = sb(lay, "q_max", [TT, 8])
        max_hi = sb(lay, "max_hi", [8, TT], F32R)
        max_lo = sb(lay, "max_lo", [8, TT], F32R)
        v = sb(lay, "v", [SK, NK, D])
        probs = [sb(lay, f"probs{i}", [SK, 4, 2 * T]) for i in range(2)]
        psum_keys = sb(lay, "psum_keys", [SK, 4, T])
        inv_den = sb(lay, "inv_den", [P, T])
        o_T = sb(lay, "o_T", [P, G, T])
        logits = sb(lay, "logits", [E, T])
        top8 = sb(lay, "top8", [E, 8])
        neg_top = sb(lay, "neg_top", [E, 1])
        beaten = sb(lay, "beaten", [E, T])
        chosen = beaten
        expo = sb(lay, "expo", [E, T])
        expo_sum = sb(lay, "expo_sum", [E, 1])
        inv_sum = sb(lay, "inv_sum", [E, 1])
        weight = sb(lay, "weight", [P, T])
        weight_T = sb(lay, "weight_T", [TT, 2, E])
        merged = sb(lay, "merged", [P, D])

        x_loaded = sem("x_loaded")
        ctx_loaded = sem("ctx_loaded")
        work_full = sem("work_full")
        xt_ready = sem("xt_ready")
        mixed = sem("mixed")
        scanned = sem("scanned")
        x1_ready = sem("x1_ready")
        yt_ready = sem("yt_ready")
        ctx_ready = sem("ctx_ready")
        q_hi_ready = sem("q_hi_ready")
        q_ready = sem("q_ready")
        k_hi_ready = sem("k_hi_ready")
        k_ready = sem("k_ready")
        v_ready = sem("v_ready")
        x2_ready = sem("x2_ready")
        rt_ready = sem("rt_ready")
        logits_ready = sem("logits_ready")
        wt_ready = sem("wt_ready")
        merged_ready = sem("merged_ready")
        mt_ready = sem("mt_ready")
        k_stacked = [sem(f"k_stacked{i}") for i in range(G)]
        q_stacked = [sem(f"q_stacked{i}") for i in range(G)]
        max_stacked = [sem(f"max_stacked{i}") for i in range(G)]
        s_full1 = sem("s_full1")
        s_drained = sem("s_drained")
        q_max_ready = sem("q_max_ready")
        max_hi_ready = sem("max_hi_ready")
        max_ready = sem("max_ready")
        scores_ready = sem("scores_ready")
        probs_ready = sem("probs_ready")
        pv_done = sem("pv_done")
        keys_summed = sem("keys_summed")
        pool_chain = sem("pool_chain")
        den_done = sem("den_done")
        inv_ready = sem("inv_ready")
        o_ready = sem("o_ready")
        stats_done = sem("stats_done")
        agg_done = sem("agg_done")
        eps_done = sem("eps_done")
        rstd_done = sem("rstd_done")
        xh_ready = sem("xh_ready")
        xr_ready = sem("xr_ready")
        x_bias_ready = sem("x_bias_ready")
        x1_kept_ready = sem("x1_kept_ready")
        x2_stored = sem("x2_stored")
        top8_ready = sem("top8_ready")
        neg_ready = sem("neg_ready")
        router_chain = sem("router_chain")
        expo_ready = sem("expo_ready")
        weight_ready = sem("weight_ready")
        router_stored = sem("router_stored")
        constants = sem("constants")

        OUT = {"xt0": (xt_ready, 2, 0), "xt1": (xt_ready, 2, 1), "pa": (scanned, 3, 0),
               "pc": (scanned, 3, 1), "pz": (scanned, 3, 2), "mix0": (x1_ready, 2, 0),
               "mix1": (x1_ready, 2, 1), "yt0": (yt_ready, 2, 0), "yt1": (yt_ready, 2, 1),
               "out0": (x2_ready, 2, 0), "out1": (x2_ready, 2, 1), "rt0": (rt_ready, 2, 0),
               "rt1": (rt_ready, 2, 1), "gate": (logits_ready, 1, 0), "wt0": (wt_ready, 2, 0),
               "wt1": (wt_ready, 2, 1), "merge": (merged_ready, 1, 0), "mt": (mt_ready, 1, 0)}
        for i in range(4):
            OUT[f"ct{i}"] = (ctx_ready, 4, i)
            OUT[f"q{i}"] = (q_ready, 4, i)
            for c in range(2):
                OUT[f"k{i}.{c}"] = (k_ready, 8, 2 * i + c)
        for i in range(NK):
            OUT[f"v{i}"] = (v_ready, NK, i)

        def wait_out(eng, job, b):
            s, per, i = OUT[job]
            eng.wait_ge(s, b * per + (i + 1))

        def group_before(b, kt):
            return (kt - 1, b + 1) if kt else (G - 1, b)

        def isint(b):
            return isinstance(b, int)

        def jobs_at(kind, kt, s):
            return [j for g, st_, j in TIMETABLE if (g, st_) == (kt, s) and j in SEQ[kind]]

        def bank_of(job, kind):
            return bank[place(job, kind) % 2]

        def norm_no(which, kind, b):
            if kind == "first":
                return 2 + {0: 0, 1: 1}[which]
            if kind == "mid":
                return b * 3 + {0: 1, 2: 2, 1: 3}[which]
            if kind == "last":
                return LAST * 3 + 1
            return 3 * B - 1

        def chunk(c):
            return slice(SC[c], SC[c + 1])

        def batches(eng, step):
            step("pro", -1)
            step("first", 0)
            with eng.Fori(1, LAST) as b:
                step("mid", b)
            step("last", LAST)
            step("tail", LAST + 1)

        with nc.Block() as block:
            @block.sync
            def _(sp):
                def value(x):
                    return x if isint(x) else sp.snap(x)

                def load_x(b):
                    b = value(b)
                    if not isint(b) or b >= 1:
                        sp.wait_ge(x1_ready, b * 2)
                    sp.dma_start(x_in[:], x[b, :, :].rearrange("(t p) d -> p t d", p=TT)
                                 if isint(b) else x[bass.ds(b, 1), :, :].rearrange(
                                     "o (t p) d -> p (o t) d", p=TT)).then_inc(x_loaded, 16)

                def load_ctx(b):
                    b = value(b)
                    if not isint(b) or b >= 1:
                        sp.wait_ge(ctx_ready, b * 4)
                    sp.dma_start(ctx_nat[:], ctx_in[b, :, :].rearrange("(k p) d -> p k d", p=SK)
                                 if isint(b) else ctx_in[bass.ds(b, 1), :, :].rearrange(
                                     "o (k p) d -> p (o k) d", p=SK)).then_inc(ctx_loaded, 16)

                def stack(b, kt):
                    slot = kt
                    q_count = value(b * 4 + (kt + 1))
                    k_count = value(b * 8 + 2 * (kt + 1))
                    sp.wait_ge(q_ready, q_count)
                    for j in range(4):
                        src = slice(j * HD, (j + 1) * HD)
                        for r, part in enumerate((q_hi, q_hi, q_lo)):
                            sp.dma_start(q_st[slot][r * HD:(r + 1) * HD, j, :].bitcast(F32),
                                         part[src, :].bitcast(F32)).then_inc(q_stacked[slot], 16)
                    sp.wait_ge(k_ready, k_count)
                    for j in range(4):
                        src = slice(j * HD, (j + 1) * HD)
                        for r, part in enumerate((k_hi, k_lo, k_hi)):
                            sp.dma_start(k_st[slot][r * HD:(r + 1) * HD, j, :].bitcast(F32),
                                         part[src, :].bitcast(F32)).then_inc(k_stacked[slot], 16)

                def store(b):
                    sp.wait_ge(x2_ready, b * 2 + 2)
                    dst = out[b, :, :].rearrange("(t p) d -> p t d", p=TT) if isint(b) else \
                        out[bass.ds(b, 1), :, :].rearrange("o (t p) d -> p (o t) d", p=TT)
                    sp.dma_start(dst, x2[:]).then_inc(x2_stored, 16)

                def keep_weight(b):
                    sp.wait_ge(weight_ready, b + 1)
                    sp.dma_start(router[bass.ds(b, 1), :, :].rearrange("o e t -> e (o t)"),
                                 weight[0:E, :]).then_inc(router_stored, 16)

                def step(kind, b):
                    if kind == "pro":
                        load_x(0)
                        load_ctx(0)
                        stack(0, 0)
                        stack(0, 1)
                        return
                    if kind == "tail":
                        store(b - 1)
                        keep_weight(b - 1)
                        return
                    if kind != "last":
                        load_x(b + 1)
                    for kt in range(4):
                        if kt < 2:
                            stack(b, kt + 2)
                        elif kind != "last":
                            stack(b + 1, kt - 2)
                        if kt == 0 and kind != "last":
                            load_ctx(b + 1)
                        if kt == 2 and kind != "first":
                            store(b - 1)
                        if kt == 3 and kind != "first":
                            keep_weight(b - 1)

                batches(sp, step)
                sp.wait_ge(x2_stored, 16 * B)
                sp.wait_ge(router_stored, 16 * B)

            @block.gpsimd
            def _(pool):
                nc.gpsimd.memset(weight[:], 0.0).then_inc(constants, 1)
                nc.gpsimd.memset(merged[:], 0.0).then_inc(constants, 1)
                pool.wait_ge(constants, 2)
                for i in range(G):
                    nc.gpsimd.memset(k_st[i][3 * HD:3 * HD + 2, :, :].bitcast(F32), 1.0
                                     ).then_inc(constants, 1)
                pool.wait_ge(constants, 6)

                def root(which, n):
                    pool.drain()
                    pool.wait_ge(agg_done, n * 2 + 2)
                    nc.gpsimd.tensor_tensor(rstd[:, which, :], mean_var[:, which, :, 1],
                                            eps_tile[0:TT, :], ALU.add).then_inc(eps_done, 1)
                    pool.wait_ge(eps_done, n + 1)
                    nc.gpsimd.tensor_tensor(rstd[:, which, :], rstd[:, which, :],
                                            halves[0:TT, :], ALU.pow).then_inc(rstd_done, 1)

                def bias(b):
                    pool.drain()
                    pool.wait_ge(xh_ready, b * 4 + 2)
                    nc.gpsimd.tensor_tensor(x_in[:], x_in[:],
                                            bias_row[:].unsqueeze(1).to_broadcast([TT, 2, D]),
                                            ALU.add).then_inc(x_bias_ready, 1)

                def keep(b):
                    pool.drain()
                    pool.wait_ge(x1_ready, b * 2 + 2)
                    if not (isint(b) and b == 0):
                        pool.wait_ge(x2_ready, b * 2)
                    nc.gpsimd.tensor_tensor(
                        x1_kept[:], x1[:], ones[0:TT, 0:1].unsqueeze(2).to_broadcast([TT, 2, D]),
                        ALU.mult).then_inc(x1_kept_ready, 1)

                def sum_keys(b, kt, c):
                    p = probs[(3 * kt + c) % 2]
                    pool.drain()
                    pool.wait_ge(probs_ready, (b * 4 + kt) * 12 + (4 * c + 4))
                    lo, hi = p[:, :, 0:T], p[:, :, T:2 * T]
                    if c == 0:
                        if not (isint(b) and b == 0 and kt == 0):
                            pool.wait_ge(den_done, b * 4 + kt)
                        nc.gpsimd.tensor_tensor(psum_keys[:], lo, hi, ALU.add
                                                ).then_inc(keys_summed, 1)
                        return
                    pool.wait_ge(keys_summed, (b * 4 + kt) * 3 + c)
                    nc.gpsimd.tensor_tensor(psum_keys[:], psum_keys[:], lo, ALU.add
                                            ).then_inc(pool_chain, 1)
                    pool.wait_ge(pool_chain, (b * 4 + kt) * 2 + c)
                    nc.gpsimd.tensor_tensor(psum_keys[:], psum_keys[:], hi, ALU.add
                                            ).then_inc(keys_summed, 1)

                def step(kind, b):
                    if kind == "pro":
                        root(0, 0)
                        bias(0)
                        root(1, 1)
                        return
                    if kind == "tail":
                        root(2, 3 * B - 1)
                        return
                    for kt in range(4):
                        for s in range(STEPS):
                            if (kt, s) == (1, 1):
                                keep(b)
                            if (kt, s) == (0, 6) and kind != "last":
                                root(0, norm_no(0, kind, b))
                            if (kt, s) == (1, 0) and kind != "last":
                                bias(b + 1)
                            if (kt, s) == (1, 6) and kind != "first":
                                root(2, norm_no(2, kind, b))
                            if (kt, s) == (1, 12) and kind != "last":
                                root(1, norm_no(1, kind, b))
                            if s in SUM_AT:
                                sum_keys(b, kt, SUM_AT[s])

                batches(pool, step)

            @block.scalar
            def _(act):
                def fill(job, kind, b):
                    bb = batch_of(job, kind, b)
                    ps = bank_of(job, kind)
                    s, per, i = OUT[job]
                    full = number(job, kind, b) + 1
                    if job[:2] in ("xt", "yt", "rt"):
                        dst = {"xt": xT, "yt": yT, "rt": rT}[job[:2]]
                        act.wait_ge(work_full, full)
                        nc.scalar.copy(dst[:, 2 * i:2 * i + 2, :].rearrange("p k n -> p (k n)"),
                                       ps[:, 0:2 * T]).then_inc(s, 1)
                    elif job[:2] == "ct":
                        kc, half = i % 2, i // 2
                        act.wait_ge(work_full, full)
                        nc.scalar.copy(ctx_T[:, kc, half * 3 * SK:(half + 1) * 3 * SK],
                                       ps[:, 0:3 * SK]).then_inc(s, 1)
                    elif job[0] == "q":
                        if not (isint(bb) and bb == 0 and i == 0):
                            slot, n = group_before(bb, i)
                            act.wait_ge(q_stacked[slot], n * 192)
                        act.wait_ge(work_full, full)
                        nc.scalar.copy(q_hi[:], ps[:, 0:T]).then_inc(q_hi_ready, 1)
                    elif job[0] == "k":
                        kt, c = i // 2, i % 2
                        if c == 0 and not (isint(bb) and bb == 0 and kt == 0):
                            slot, n = group_before(bb, kt)
                            act.wait_ge(k_stacked[slot], n * 192)
                        act.wait_ge(work_full, full)
                        nc.scalar.copy(k_hi[:, chunk(c)], ps[:, 0:SC[c + 1] - SC[c]]
                                       ).then_inc(k_hi_ready, 1)
                    elif job[0] == "v":
                        act.wait_ge(work_full, full)
                        nc.scalar.copy(v[:, i, :], ps[0:SK, :]).then_inc(s, 1)
                    elif job == "gate":
                        act.wait_ge(work_full, full)
                        nc.scalar.activation(logits[:], ps[0:E, 0:T], ACT.Identity,
                                             bias=gate_bias[:, 0:1]).then_inc(s, 1)
                    elif job[:2] == "wt":
                        act.wait_ge(work_full, full)
                        nc.scalar.copy(weight_T[:, i, :], ps[0:TT, 0:E]).then_inc(s, 1)
                    elif job == "merge":
                        if isint(bb) or kind == "mid":
                            act.wait_ge(constants, 4)
                        act.wait_ge(work_full, full)
                        nc.scalar.copy(merged[0:E, :], ps[0:E, :]).then_inc(s, 1)

                def router_exp(b):
                    act.wait_ge(neg_ready, b + 1)
                    nc.scalar.activation(expo[:], logits[:], ACT.Exp, bias=neg_top[:, 0:1],
                                         accum_out=expo_sum[:]).then_inc(expo_ready, 1)

                def exp(b, kt, u):
                    c, j = u // 4, u % 4
                    n = 3 * kt + c
                    if not (isint(b) and b == 0 and n < 2):
                        act.wait_ge(pv_done, b * 12 + (n - 1))
                        act.wait_ge(keys_summed, b * 12 + (n - 1))
                    act.wait_ge(scores_ready, (b * 4 + kt) * 12 + (u + 1))
                    nc.scalar.activation(probs[n % 2][:, j, :], bank[5 + u % 2][0:SK, 0:2 * T],
                                         ACT.Exp, scale=SCALE).then_inc(probs_ready, 1)

                def stack_max(b, kt):
                    slot = kt
                    act.wait_ge(max_ready, b * 4 + (kt + 1))
                    for r, part in enumerate((max_hi, max_lo)):
                        row = 3 * HD + r
                        act.dma_start(q_st[slot][row:row + 1, :, :].rearrange(
                            "o j (t n) -> o (j t) n", t=2).bitcast(F32), part[:, :].bitcast(F32)
                                     ).then_inc(max_stacked[slot], 16)

                def step(kind, b):
                    if kind in ("pro", "tail"):
                        for job in SEQ[kind]:
                            fill(job, kind, b)
                            if job == "gate":
                                router_exp(b - 1)
                        if kind == "pro":
                            stack_max(0, 0)
                        return
                    for kt in range(4):
                        for s in range(STEPS):
                            for job in jobs_at(kind, kt, s):
                                fill(job, kind, b)
                            if (kt, s) == (2, 10) and kind != "first":
                                router_exp(b - 1)
                            if 0 <= s - UNIT_AT < 12:
                                exp(b, kt, s - UNIT_AT)
                            if s == ROWS_AT and kt < 3:
                                stack_max(b, kt + 1)
                            elif s == ROWS_AT and kind != "last":
                                stack_max(b + 1, 0)

                batches(act, step)

            @block.vector
            def _(dve):

                def relay_wait(b, place):
                    if not isint(b):
                        nc.vector.tensor_copy(relay[0:1, place + 1:place + 2], relay[0:1, 0:1])

                def norm_stats(which, n, src):
                    for t in range(2):
                        nc.vector.bn_stats(stats[:, which, t, :], src[:, t, :]
                                           ).then_inc(stats_done, 1)
                    for t in range(2):
                        dve.wait_ge(stats_done, n * 2 + (t + 1))
                        relay_wait(n, which * 2 + t)
                        nc.vector.bn_aggr(mean_var[:, which, t, :], stats[:, which, t, :]
                                          ).then_inc(agg_done, 1)

                def norm_apply(which, n, src, dst, s):
                    dve.wait_ge(rstd_done, n + 1)
                    for t in range(2):
                        nc.vector.tensor_scalar(dst[:, t, :], src[:, t, :],
                                                mean_var[:, which, t, 0:1],
                                                rstd[:, which, t:t + 1],
                                                ALU.subtract, ALU.mult).then_inc(s, 1)

                def mixer_stats(b, n):
                    dve.wait_ge(x_loaded, b * 16 + 16)
                    norm_stats(0, n, x_in)

                def mixer_apply(b, n):
                    if not (isint(b) and b == 0):
                        dve.wait_ge(yt_ready, b * 2)
                    norm_apply(0, n, x_in, xh, xh_ready)

                def attention_stats(b, n):
                    dve.wait_ge(x1_ready, b * 2 + 2)
                    norm_stats(1, n, x1)

                def attention_apply(b, n):
                    dve.wait_ge(xt_ready, b * 2 + 2)
                    norm_apply(1, n, x1, xh, xh_ready)

                def router_stats(b, n):
                    dve.wait_ge(x2_ready, b * 2 + 2)
                    norm_stats(2, n, x2)

                def router_apply(b, n):
                    norm_apply(2, n, x2, xr, xr_ready)

                def fill(job, kind, b):
                    bb = batch_of(job, kind, b)
                    ps = bank_of(job, kind)
                    s, per, i = OUT[job]
                    full = number(job, kind, b) + 1
                    if job == "pa":
                        dve.wait_ge(work_full, full)
                        nc.vector.tensor_tensor(
                            a_mix[:], ps[:, 0:2 * T].rearrange("p (g n) -> p g n", g=2),
                            inv_count[:].unsqueeze(1).to_broadcast([P, 2, T]), ALU.mult
                        ).then_inc(s, 1)
                    elif job == "pc":
                        dve.wait_ge(work_full, full)
                        nc.vector.tensor_tensor_scan(c_mix[:, 0, :], ones[:], ps[:, 0:T], 0.0,
                                                     ALU.mult, ALU.add).then_inc(mixed, 1)
                        nc.vector.tensor_tensor_scan(c_mix[:, 1, :], ones[:], ps[:, T:2 * T], 0.0,
                                                     ALU.mult, ALU.add).then_inc(s, 1)
                    elif job == "pz":
                        dve.wait_ge(work_full, full)
                        nc.vector.tensor_tensor_scan(z_mix[:], ones[:], ps[:, 0:T], 0.0,
                                                     ALU.mult, ALU.add).then_inc(s, 1)
                        dve.wait_ge(scanned, bb * 3 + 2)
                        dve.wait_ge(mixed, bb * 4 + 1)
                        nc.vector.tensor_tensor(g_mix[:], a_mix[:], c_mix[:], ALU.mult
                                                ).then_inc(mixed, 1)
                        dve.wait_ge(scanned, bb * 3 + 3)
                        nc.vector.tensor_tensor(z_mix[:], z_mix[:], inv_count[:], ALU.mult
                                                ).then_inc(mixed, 1)
                        dve.wait_ge(mixed, bb * 4 + 3)
                        nc.vector.tensor_tensor(g_mix[:, 1, :], g_mix[:, 1, :], z_mix[:],
                                                ALU.mult).then_inc(mixed, 1)
                    elif job[:3] == "mix":
                        if i == 0:
                            dve.wait_ge(x_bias_ready, bb + 1)
                            if not (isint(bb) and bb == 0):
                                dve.wait_ge(x1_kept_ready, bb)
                        dve.wait_ge(work_full, full)
                        nc.vector.tensor_tensor(x1[:, i, :], ps[0:TT, :], x_in[:, i, :],
                                                ALU.add).then_inc(s, 1)
                    elif job[0] == "q":
                        dve.wait_ge(work_full, full)
                        dve.wait_ge(q_hi_ready, bb * 4 + (i + 1))
                        nc.vector.tensor_tensor(q_lo[:], ps[:, 0:T], q_hi[:].bitcast(F32),
                                                ALU.subtract).then_inc(s, 1)
                    elif job[0] == "k":
                        c = i % 2
                        dve.wait_ge(work_full, full)
                        dve.wait_ge(k_hi_ready, bb * 8 + (i + 1))
                        nc.vector.tensor_tensor(k_lo[:, chunk(c)], ps[:, 0:SC[c + 1] - SC[c]],
                                                k_hi[:, chunk(c)].bitcast(F32), ALU.subtract
                                                ).then_inc(s, 1)
                    elif job[:3] == "out":
                        if i == 0:
                            dve.wait_ge(x1_kept_ready, bb + 1)
                            if not (isint(bb) and bb == 0):
                                dve.wait_ge(x2_stored, bb * 16)
                        dve.wait_ge(work_full, full)
                        nc.vector.tensor_tensor(x2[:, i, :], ps[0:TT, :], x1_kept[:, i, :],
                                                ALU.add).then_inc(s, 1)
                    elif job == "mt":
                        dve.wait_ge(work_full, full)
                        nc.vector.tensor_copy(
                            merged_T[:, :, :, bass.ds(bb, 1)],
                            ps[:].rearrange("p (k e o) -> p k e o", k=KD, o=1)[:, :, 0:E, :]
                        ).then_inc(s, 1)

                def router_top(b):
                    dve.wait_ge(logits_ready, b + 1)
                    relay_wait(b, 6)
                    nc.vector.max(top8[:], logits[:]).then_inc(top8_ready, 1)
                    dve.wait_ge(top8_ready, b + 1)
                    nc.vector.tensor_scalar(neg_top[:], top8[:, 0:1], -1.0, None, ALU.mult
                                            ).then_inc(neg_ready, 1)
                    nc.vector.match_replace(beaten[:], top8[:], logits[:], NEG
                                            ).then_inc(router_chain, 1)
                    dve.wait_ge(router_chain, b * 3 + 1)
                    nc.vector.tensor_tensor(chosen[:], logits[:], beaten[:], ALU.not_equal
                                            ).then_inc(router_chain, 1)

                def router_weight(b):
                    dve.wait_ge(expo_ready, b + 1)
                    if isint(b) and b == 0:
                        dve.wait_ge(constants, 4)
                    nc.vector.reciprocal(inv_sum[:], expo_sum[:]).then_inc(router_chain, 1)
                    dve.wait_ge(router_chain, b * 3 + 3)
                    if not (isint(b) and b == 0):
                        dve.wait_ge(router_stored, b * 16)
                    nc.vector.scalar_tensor_tensor(out=weight[0:E, :], in0=expo[:], scalar=inv_sum[:, 0:1],
                                                   in1=chosen[:], op0=ALU.mult, op1=ALU.mult
                                                   ).then_inc(weight_ready, 1)

                def take_max(b, kt, n):
                    j, t, c = n // 4, n // 2 % 2, n % 2
                    g17 = (b * 4 + kt) * 17
                    dve.wait_ge(s_full1, g17 + (n + 1))
                    nc.vector.tensor_reduce(maxes[:, j, t, c:c + 1],
                                            bank[2 + n % 3][0:TT, 0:SC[c + 1] - SC[c]], AX.X,
                                            ALU.max).then_inc(s_drained, 1)

                def join_maxima(b, kt):
                    g = b * 4 + kt
                    dve.wait_ge(s_drained, g * 16 + 16)
                    nc.vector.tensor_reduce(q_max[:], maxes[:].rearrange("p j t c -> p (j t) c"),
                                            AX.X, ALU.max).then_inc(q_max_ready, 1)

                def max_rows(b, kt):
                    g = b * 4 + kt
                    dve.wait_ge(s_full1, g * 17 + 17)
                    if not (isint(b) and b == 0 and kt == 0):
                        slot, n = group_before(b, kt)
                        dve.wait_ge(max_stacked[slot], n * 32)
                    nc.vector.tensor_scalar(max_hi[:], bank[2][0:8, 0:TT], -1.0, None, ALU.mult
                                            ).then_inc(max_hi_ready, 1)
                    dve.wait_ge(max_hi_ready, g + 1)
                    nc.vector.scalar_tensor_tensor(out=max_lo[:], in0=bank[2][0:8, 0:TT],
                                                   scalar=-1.0, in1=max_hi[:].bitcast(F32),
                                                   op0=ALU.mult, op1=ALU.subtract
                                                   ).then_inc(max_ready, 1)

                def normalise(b, kt):
                    g = b * 4 + kt
                    dve.wait_ge(den_done, g + 1)
                    nc.vector.reciprocal(inv_den[:], bank[7][:, T:2 * T]).then_inc(inv_ready, 1)
                    dve.wait_ge(inv_ready, g + 1)
                    nc.vector.tensor_tensor(o_T[:, kt, :], bank[7][:, 0:T], inv_den[:], ALU.mult
                                            ).then_inc(o_ready, 1)

                def step(kind, b):
                    if kind == "pro":
                        mixer_stats(0, 0)
                        mixer_apply(0, 0)
                        for job in SEQ[kind]:
                            fill(job, kind, b)
                            if job == "mix1":
                                attention_stats(0, 1)
                                attention_apply(0, 1)
                        for n in range(16):
                            take_max(0, 0, n)
                        join_maxima(0, 0)
                        max_rows(0, 0)
                        return
                    if kind == "tail":
                        normalise(b - 1, G - 1)
                        for job in SEQ[kind]:
                            fill(job, kind, b)
                            if job == "out1":
                                router_stats(b - 1, norm_no(2, kind, b))
                                router_apply(b - 1, norm_no(2, kind, b))
                            if job == "gate":
                                router_top(b - 1)
                                router_weight(b - 1)
                        return
                    for kt in range(4):
                        nb, nk = (b, kt + 1) if kt < 3 else (b + 1, 0)
                        more = not (kt == 3 and kind == "last")
                        for s in range(STEPS):
                            if more and s == TURN_AT:
                                join_maxima(nb, nk)
                            if more:
                                for n in maxima_at(kt, s)[:1]:
                                    take_max(nb, nk, n)
                            for job in jobs_at(kind, kt, s):
                                fill(job, kind, b)
                            if more:
                                for n in maxima_at(kt, s)[1:]:
                                    take_max(nb, nk, n)
                            if kt == 0 and kind != "last":
                                if s == 6:
                                    mixer_stats(b + 1, norm_no(0, kind, b))
                                if s == 8:
                                    mixer_apply(b + 1, norm_no(0, kind, b))
                            if kt == 1 and kind != "first":
                                if s == 5:
                                    router_stats(b - 1, norm_no(2, kind, b))
                                if s == 7:
                                    router_apply(b - 1, norm_no(2, kind, b))
                            if kind != "last":
                                if (kt, s) == (1, 11):
                                    attention_stats(b + 1, norm_no(1, kind, b))
                                if (kt, s) == (1, 13):
                                    attention_apply(b + 1, norm_no(1, kind, b))
                            if kind != "first":
                                if (kt, s) == (2, 10):
                                    router_top(b - 1)
                                if (kt, s) == (2, 11):
                                    router_weight(b - 1)
                            if s == LATE_AT + 1:
                                if kt:
                                    normalise(b, kt - 1)
                                elif kind != "first":
                                    normalise(b - 1, G - 1)
                            if more and s == TURN_AT + 1:
                                max_rows(nb, nk)

                batches(dve, step)

            @block.tensor
            def _(pe):

                def fill(job, kind, b):
                    bb = batch_of(job, kind, b)
                    ps = bank_of(job, kind)
                    s, per, i = OUT[job]
                    prev = before(job, kind, b)
                    if prev:
                        wait_out(pe, *prev)
                    if job[:2] in ("xt", "yt", "rt"):
                        src = xr if job[0] == "r" else xh
                        if job[:2] == "xt":
                            pe.wait_ge(xh_ready, bb * 4 + 2)
                        elif job[:2] == "yt":
                            pe.wait_ge(xh_ready, bb * 4 + 4)
                        else:
                            pe.wait_ge(xr_ready, bb * 2 + 2)
                        for kk in range(2):
                            for t in range(2):
                                kd = 2 * i + kk
                                last = nc.tensor.transpose(
                                    ps[:, kk * T + t * TT:kk * T + (t + 1) * TT],
                                    src[:, t, kd * P:(kd + 1) * P], ident[0:TT, 0:TT])
                    elif job[:2] == "ct":
                        kc, half = i % 2, i // 2
                        pe.wait_ge(ctx_loaded, bb * 16 + 16)
                        for k in range(3):
                            last = nc.tensor.transpose(
                                ps[:, k * SK:(k + 1) * SK],
                                ctx_nat[:, half * 3 + k, kc * P:(kc + 1) * P], ident[0:SK, 0:SK])
                    elif job in ("pa", "pc", "pz"):
                        w = {"pa": in_q, "pc": in_k, "pz": in_z}[job]
                        pe.wait_ge(xt_ready, bb * 2 + 2)
                        for g in range(1 if job == "pz" else 2):
                            for kd in range(KD):
                                last = nc.tensor.matmul(ps[:, g * T:(g + 1) * T],
                                                        w[:, kd, g * R:(g + 1) * R], xT[:, kd, :],
                                                        start=(kd == 0), stop=(kd == KD - 1))
                    elif job[:3] == "mix":
                        pe.wait_ge(mixed, bb * 4 + 4)
                        for g in range(2):
                            last = nc.tensor.matmul(ps[0:TT, :], g_mix[:, g, i * TT:(i + 1) * TT],
                                                    mix_out[:, g, :], start=(g == 0), stop=(g == 1))
                    elif job[0] == "q":
                        pe.wait_ge(yt_ready, bb * 2 + 2)
                        for kd in range(KD):
                            last = nc.tensor.matmul(ps[:, 0:T], wq_T[:, kd, i * P:(i + 1) * P],
                                                    yT[:, kd, :], start=(kd == 0),
                                                    stop=(kd == KD - 1))
                    elif job[0] == "k":
                        kt, c = i // 2, i % 2
                        pe.wait_ge(ctx_ready, bb * 4 + 4)
                        for kc in range(KC):
                            last = nc.tensor.matmul(ps[:, 0:SC[c + 1] - SC[c]],
                                                    wk_T[:, kc, kt * P:(kt + 1) * P],
                                                    ctx_T[:, kc, chunk(c)], start=(kc == 0),
                                                    stop=(kc == KC - 1))
                    elif job[0] == "v":
                        pe.wait_ge(ctx_ready, bb * 4 + 4)
                        for kc in range(KC):
                            last = nc.tensor.matmul(ps[0:SK, :], ctx_T[:, kc, i * SK:(i + 1) * SK],
                                                    wv_T[:, kc, :], start=(kc == 0),
                                                    stop=(kc == KC - 1))
                    elif job[:3] == "out":
                        pe.wait_ge(o_ready, bb * 4 + 4)
                        for kt in range(G):
                            last = nc.tensor.matmul(ps[0:TT, :], o_T[:, kt, i * TT:(i + 1) * TT],
                                                    wo_T[:, kt, :], start=(kt == 0),
                                                    stop=(kt == G - 1))
                    elif job == "gate":
                        pe.wait_ge(rt_ready, bb * 2 + 2)
                        for kd in range(KD):
                            last = nc.tensor.matmul(ps[0:E, 0:T], gate_T[:, kd, :], rT[:, kd, :],
                                                    start=(kd == 0), stop=(kd == KD - 1))
                    elif job[:2] == "wt":
                        pe.wait_ge(weight_ready, bb + 1)
                        last = nc.tensor.transpose(ps[0:TT, 0:P], weight[:, i * TT:(i + 1) * TT],
                                                   ident[:])
                    elif job == "merge":
                        pe.wait_ge(wt_ready, bb * 2 + 2)
                        for t in range(2):
                            last = nc.tensor.matmul(ps[0:E, :], weight_T[:, t, :], xr[:, t, :],
                                                    start=(t == 0), stop=(t == 1))
                    elif job == "mt":
                        pe.wait_ge(merged_ready, bb + 1)
                        for kd in range(KD):
                            last = nc.tensor.transpose(ps[:, kd * P:(kd + 1) * P],
                                                       merged[:, kd * P:(kd + 1) * P],
                                                       ident[:])
                    last.then_inc(work_full, 1)

                def scores(b, kt, n):
                    j, t, c = n // 4, n // 2 % 2, n % 2
                    slot = kt
                    if n == 0:
                        pe.wait_ge(q_stacked[slot], b * 192 + 192)
                        pe.wait_ge(k_stacked[slot], b * 192 + 192)
                        if not (isint(b) and b == 0 and kt == 0):
                            pe.wait_ge(max_ready, b * 4 + kt)
                    elif n >= 3:
                        pe.wait_ge(s_drained, (b * 4 + kt) * 16 + (n - 2))
                    nc.tensor.matmul(bank[2 + n % 3][0:TT, 0:SC[c + 1] - SC[c]],
                                     q_st[slot][0:3 * HD, j, t * TT:(t + 1) * TT],
                                     k_st[slot][0:3 * HD, j, chunk(c)],
                                     start=True, stop=True).then_inc(s_full1, 1)

                def turn_max(b, kt):
                    pe.wait_ge(q_max_ready, b * 4 + (kt + 1))
                    nc.tensor.transpose(bank[2][0:8, 0:TT], q_max[:], ident[0:TT, 0:TT]
                                        ).then_inc(s_full1, 1)

                def scores_T(b, kt, u):
                    c, j = u // 4, u % 4
                    slot = kt
                    n = (b * 4 + kt) * 12 + u
                    if u == 0:
                        pe.wait_ge(max_stacked[slot], b * 32 + 32)
                        if isint(b) and b == 0:
                            pe.wait_ge(constants, 6)
                    if not (isint(b) and b == 0 and kt == 0 and u < 2):
                        pe.wait_ge(probs_ready, (b * 4 + kt) * 12 + (u - 1))
                    for kk in range(2):
                        k = 2 * c + kk
                        last = nc.tensor.matmul(bank[5 + u % 2][0:SK, kk * T:(kk + 1) * T],
                                                k_st[slot][:, j, k * SK:(k + 1) * SK],
                                                q_st[slot][:, j, :], start=True, stop=True)
                    last.then_inc(scores_ready, 1)

                def values(b, kt, c):
                    p = probs[(3 * kt + c) % 2]
                    if c == 0:
                        if not (isint(b) and b == 0 and kt == 0):
                            pe.wait_ge(o_ready, b * 4 + kt)
                    if kt == 0:
                        pe.wait_ge(v_ready, b * NK + 2 * (c + 1))
                    pe.wait_ge(probs_ready, (b * 4 + kt) * 12 + (4 * c + 4))
                    for kk in range(2):
                        for j in range(4):
                            col = kt * P + j * HD
                            last = nc.tensor.matmul(bank[7][j * HD:(j + 1) * HD, 0:T],
                                                    v[:, 2 * c + kk, col:col + HD],
                                                    p[:, j, kk * T:(kk + 1) * T],
                                                    start=(c == 0 and kk == 0),
                                                    stop=(c == 2 and kk == 1))
                    last.then_inc(pv_done, 1)

                def denominators(b, kt):
                    pe.wait_ge(keys_summed, (b * 4 + kt) * 3 + 3)
                    for j in range(4):
                        last = nc.tensor.matmul(bank[7][j * HD:(j + 1) * HD, T:2 * T],
                                                ones[0:SK, 0:HD], psum_keys[:, j, :],
                                                start=True, stop=True)
                    last.then_inc(den_done, 1)

                def last_values(kind, b, kt):
                    if kt:
                        values(b, kt - 1, 2)
                    elif kind != "first":
                        values(b - 1, G - 1, 2)

                def step(kind, b):
                    if kind in ("pro", "tail"):
                        if kind == "tail":
                            values(b - 1, G - 1, 2)
                            denominators(b - 1, G - 1)
                        for job in SEQ[kind]:
                            fill(job, kind, b)
                        if kind == "pro":
                            for n in range(16):
                                scores(0, 0, n)
                            turn_max(0, 0)
                        return
                    for kt in range(4):
                        nb, nk = (b, kt + 1) if kt < 3 else (b + 1, 0)
                        more = not (kt == 3 and kind == "last")
                        for s in range(STEPS):
                            if s == LAST_PV_AT:
                                last_values(kind, b, kt)
                            if more:
                                for n in maxima_at(kt, s)[:1]:
                                    scores(nb, nk, n)
                            for job in jobs_at(kind, kt, s):
                                fill(job, kind, b)
                            if 0 <= s - UNIT_AT < 12:
                                scores_T(b, kt, s - UNIT_AT)
                            if more:
                                for n in maxima_at(kt, s)[1:]:
                                    scores(nb, nk, n)
                            if s == TURN_AT + 1 and more:
                                turn_max(nb, nk)
                            if s == LATE_AT:
                                if kt:
                                    denominators(b, kt - 1)
                                elif kind != "first":
                                    denominators(b - 1, G - 1)
                            if s in PV_AT:
                                values(b, kt, PV_AT[s])

                batches(pe, step)
        lay.close()

        D1, H1 = KD * P, H
        HC = H // BANK
        HT = BANK // P
        SLOTS = 8
        ring = sb(es, "ring", [P, SLOTS, 2 * H])
        tok = sb(es, "tok", [P, 2, KD, 32])
        hid = sb(es, "hid", [P, 2, BANK])
        hid_T = sb(es, "hid_T", [P, 2, HT, P])
        b1_rows = sb(es, "b1_rows", [P, 4, P])
        b1_T = sb(es, "b1_T", [P, E, HC, HT])
        b2_wide = sb(es, "b2_wide", [P, 2, D])
        o_sb = sb(es, "o_sb", [P, 2, D])
        fin = [sb(es, f"fin{i}", [TT, 2, D]) for i in range(2)]
        o_in = [sb(es, f"o_in{i}", [P, D]) for i in range(2)]
        pick_now = [sb(es, f"pick_now{i}", [P, T]) for i in range(2)]

        chunk_in = [sem(f"chunk_in{i}") for i in range(SLOTS)]
        b1_loaded = sem("b1_loaded")
        b1_flipped = sem("b1_flipped")
        b1_ready = sem("b1_ready")
        cleared = sem("cleared")
        b2_loaded = [sem(f"b2_loaded{i}") for i in range(2)]
        tok_ready = sem("tok_ready")
        h_full = sem("h_full")
        h_out = sem("h_out")
        ht_full = sem("ht_full")
        ht_biased = sem("ht_biased")
        ht_ready = sem("ht_ready")
        o_full = sem("o_full")
        o_out = sem("o_out")
        o_stored = [sem(f"o_stored{i}") for i in range(2)]
        fin_loaded = [sem(f"fin_loaded{i}") for i in range(2)]
        scat_full = sem("scat_full")
        fin_ready = sem("fin_ready")
        fin_stored = [sem(f"fin_stored{i}") for i in range(2)]
        NB1 = E * HC * HT // P

        with nc.Block() as block:
            @block.sync
            def _(sp):
                QB = HC * HT
                per = P // QB
                for e in range(E):
                    r = e % per * QB
                    sp.dma_start(b1_rows[r:r + QB, e // per, :],
                                 w1[e, D1, :].rearrange("(q n) -> q n", n=P)
                                 ).then_inc(b1_loaded, 16)

                def weights(i, e2, first):
                    e = i * 2 + e2
                    for q in range(4):
                        slot = e2 * 4 + q
                        if not first:
                            if q < 2:
                                sp.wait_ge(h_full, i * 2 + (e2 - 1))
                            else:
                                sp.wait_ge(o_full, i * 2 + (e2 - 1))
                        if q < 2:
                            src = w1[bass.ds(e, 1), q * 2 * P:(q + 1) * 2 * P, :].rearrange(
                                "o (k p) n -> p (o k) n", p=P)
                            dst = ring[:, slot, :].rearrange("p (k n) -> p k n", k=2)
                        else:
                            t0 = (q - 2) * 2
                            src = w2[bass.ds(e, 1), 0:H1, :].rearrange(
                                "o (c t p) n -> p (o c) t n", t=HT, p=P)[:, :, t0:t0 + 2, :]
                            dst = ring[:, slot, :].rearrange("p (c t n) -> p c t n", c=HC, t=2)
                        for cc in range(1 if q < 2 else HC):
                            s_, d_ = (src, dst) if q < 2 else (src[:, cc], dst[:, cc])
                            sp.dma_start(d_, s_).then_inc(chunk_in[slot], 16)
                    if not first:
                        sp.wait_ge(o_out, i * 2 + (e2 - 1))
                    else:
                        sp.wait_ge(cleared, 2)
                    sp.dma_start(b2_wide[0:B, e2, :],
                                 w2[bass.ds(e, 1), H1, :].to_broadcast([B, D])
                                 ).then_inc(b2_loaded[e2], 16)

                weights(0, 0, True)
                weights(0, 1, True)
                with sp.Fori(1, E // 2) as i:
                    weights(i, 0, False)
                    weights(i, 1, False)

            @block.gpsimd
            def _(pool):
                nc.gpsimd.memset(b2_wide[:], 0.0).then_inc(cleared, 1)
                nc.gpsimd.memset(tok[:], 0.0).then_inc(cleared, 1)

                def keep_parts(i, e2):
                    e = i * 2 + e2
                    pool.wait_ge(o_out, i * 2 + (e2 + 1))
                    for c in range(4):
                        pool.dma_start(o_parts[:, c, bass.ds(e, 1), :].rearrange(
                            "b o n -> b (o n)"), o_sb[c * 32:c * 32 + B, e2, :]
                        ).then_inc(o_stored[e2], 16)

                with pool.Fori(0, E // 2) as i:
                    keep_parts(i, 0)
                    keep_parts(i, 1)
                for e2 in range(2):
                    pool.wait_ge(o_stored[e2], 32 * E)

            @block.scalar
            def _(act):
                def hidden(i, e2, first):
                    e = i * 2 + e2
                    act.wait_ge(h_full, e + 1)
                    if not first:
                        act.wait_ge(ht_full, e - 1)
                    nc.scalar.copy(hid[:, e2, :], bank[e2][:]).then_inc(h_out, 1)
                    act.wait_ge(ht_biased, e + 1)
                    if not first:
                        act.wait_ge(o_full, e - 1)
                    nc.scalar.activation(hid_T[:, e2].rearrange("p t m -> p (t m)"),
                                         bank[2 + e2][:], ACT.Gelu).then_inc(ht_ready, 1)

                hidden(0, 0, True)
                hidden(0, 1, True)
                with act.Fori(1, E // 2) as i:
                    hidden(i, 0, False)
                    hidden(i, 1, False)

            @block.vector
            def _(dve):
                dve.wait_ge(b1_flipped, 1)
                nc.vector.tensor_copy(b1_T[:].rearrange("p e c t -> p (e c t)"), bank[4][:]
                                      ).then_inc(b1_ready, 1)
                dve.wait_ge(cleared, 2)

                def take(i, e2, first):
                    e = i * 2 + e2
                    if not first:
                        dve.wait_ge(h_full, e - 1)
                    nc.vector.tensor_copy(tok[:, e2, :, 0:B],
                                          merged_T[:, :, bass.ds(e, 1), :].rearrange(
                                              "p k o b -> p (k o) b")).then_inc(tok_ready, 1)

                def add_biases(i, e2, first):
                    e = i * 2 + e2
                    dve.wait_ge(ht_full, e + 1)
                    if first and e2 == 0:
                        dve.wait_ge(b1_ready, 1)
                    for t in range(HT):
                        ps = bank[2 + e2][:, t * P:(t + 1) * P].rearrange("p (c m) -> p c m", c=HC)
                        last = nc.vector.tensor_tensor(
                            ps, ps, b1_T[:, bass.ds(e, 1), :, t].rearrange(
                                "p o c -> p (o c)").unsqueeze(2).to_broadcast([P, HC, 32]),
                            ALU.add)
                    last.then_inc(ht_biased, 1)

                def part_out(i, e2, first):
                    e = i * 2 + e2
                    dve.wait_ge(o_full, e + 1)
                    dve.wait_ge(b2_loaded[e2], i * 16 + 16)
                    if not first:
                        dve.wait_ge(o_stored[e2], i * 64)
                    nc.vector.tensor_tensor(o_sb[:, e2, :], bank[5 + e2][:], b2_wide[:, e2, :],
                                            ALU.add).then_inc(o_out, 1)

                def pair(i, first):
                    for e2 in range(2):
                        take(i, e2, first)
                        add_biases(i, e2, first)
                        part_out(i, e2, first)

                pair(0, True)
                with dve.Fori(1, E // 2) as i:
                    pair(i, False)

            @block.tensor
            def _(pe):
                pe.wait_ge(b1_loaded, 16 * E)
                for g in range(NB1):
                    last = nc.tensor.transpose(bank[4][:, g * P:(g + 1) * P], b1_rows[:, g, :],
                                               ident[:])
                last.then_inc(b1_flipped, 1)

                def expert(i, e2, first):
                    e = i * 2 + e2
                    pe.wait_ge(tok_ready, e + 1)
                    if not first:
                        pe.wait_ge(h_out, e - 1)
                    for kd in range(KD):
                        slot = e2 * 4 + kd // 2
                        if kd % 2 == 0:
                            pe.wait_ge(chunk_in[slot], i * 16 + 16)
                        for c in range(HC):
                            col = (kd % 2) * H + c * BANK
                            last = nc.tensor.matmul(bank[e2][c * 32:(c + 1) * 32, :],
                                                    tok[:, e2, kd, :],
                                                    ring[:, slot, col:col + BANK],
                                                    start=(kd == 0), stop=(kd == KD - 1))
                    last.then_inc(h_full, 1)
                    pe.wait_ge(h_out, e + 1)
                    if not first:
                        pe.wait_ge(ht_ready, e - 1)
                    for t in range(HT):
                        last = nc.tensor.transpose(bank[2 + e2][:, t * P:(t + 1) * P],
                                                   hid[:, e2, t * P:(t + 1) * P], ident[:])
                    last.then_inc(ht_full, 1)
                    pe.wait_ge(ht_ready, e + 1)
                    if not first:
                        pe.wait_ge(o_out, e - 1)
                    for t in range(HT):
                        slot = e2 * 4 + 2 + t // 2
                        if t % 2 == 0:
                            pe.wait_ge(chunk_in[slot], (i * 16 + 16) * HC)
                        for c in range(HC):
                            col = (c * 2 + t % 2) * D
                            last = nc.tensor.matmul(bank[5 + e2][c * 32:(c + 1) * 32, :],
                                                    hid_T[:, e2, t, c * 32:(c + 1) * 32],
                                                    ring[:, slot, col:col + D],
                                                    start=(t == 0), stop=(t == HT - 1))
                    last.then_inc(o_full, 1)

                expert(0, 0, True)
                expert(0, 1, True)
                with pe.Fori(1, E // 2) as i:
                    expert(i, 0, False)
                    expert(i, 1, False)

        with nc.Block() as block:
            @block.sync
            def _(sp):
                def load(i, slot, first):
                    b = i * 2 + slot
                    if not first:
                        sp.wait_ge(fin_stored[slot], i * 16)
                    sp.dma_start(fin[slot][:], out[bass.ds(b, 1), :, :].rearrange(
                        "o (t p) d -> p (o t) d", p=TT)).then_inc(fin_loaded[slot], 16)
                    for q in range(4):
                        sp.dma_start(pick_now[slot][q * E:(q + 1) * E, :],
                                     router[bass.ds(b, 1), :, :].rearrange("o e t -> e (o t)")
                                     ).then_inc(fin_loaded[slot], 16)
                    sp.dma_start(o_in[slot][:], o_parts[bass.ds(b, 1), :, :, :].rearrange(
                        "o c e n -> (o c e) n")).then_inc(fin_loaded[slot], 16)

                load(0, 0, True)
                load(0, 1, True)
                with sp.Fori(1, B // 2) as i:
                    load(i, 0, False)
                    load(i, 1, False)

            @block.scalar
            def _(act):
                def turn(i, slot):
                    b = i * 2 + slot
                    act.wait_ge(fin_ready, i * 4 + (slot * 2 + 2))
                    act.dma_start(out[bass.ds(b, 1), :, :].rearrange(
                        "o (t p) d -> p (o t) d", p=TT), fin[slot][:]
                    ).then_inc(fin_stored[slot], 16)

                with act.Fori(0, B // 2) as i:
                    turn(i, 0)
                    turn(i, 1)
                for slot in range(2):
                    act.wait_ge(fin_stored[slot], 16 * (B // 2))

            @block.vector
            def _(dve):
                def add(i, slot):
                    for t in range(2):
                        dve.wait_ge(scat_full, i * 4 + (slot * 2 + t + 1))
                        nc.vector.tensor_tensor(fin[slot][:, t, :], fin[slot][:, t, :],
                                                bank[slot * 2 + t][0:TT, :], ALU.add
                                                ).then_inc(fin_ready, 1)

                with dve.Fori(0, B // 2) as i:
                    add(i, 0)
                    add(i, 1)

            @block.tensor
            def _(pe):
                def scatter(i, slot, first):
                    pe.wait_ge(fin_loaded[slot], i * 96 + 96)
                    for t in range(2):
                        if not first:
                            pe.wait_ge(fin_ready, i * 4 + (slot * 2 + t - 3))
                        nc.tensor.matmul(bank[slot * 2 + t][0:TT, :],
                                         pick_now[slot][:, t * TT:(t + 1) * TT], o_in[slot][:],
                                         start=True, stop=True).then_inc(scat_full, 1)

                scatter(0, 0, True)
                scatter(0, 1, True)
                with pe.Fori(1, B // 2) as i:
                    scatter(i, 0, False)
                    scatter(i, 1, False)


_INS = ["x", "ctx_512", "L0_attn_Wq", "L0_attn_Wk", "L0_attn_Wo", "L0_attn_U_b", "L0_attn_V_b",
        "L0_attn_W_b", "L0_attn_bias_b", "L0_attn_U_t", "L0_attn_V_t", "L0_attn_W_t",
        "L0_attn_X_t", "L0_attn_bias_t", "L0_attn_alpha", "L0_xattn_Wq", "L0_xattn_Wkv",
        "L0_xattn_Wo", "L0_ffn_gate_w", "L0_ffn_gate_b", "L0_ffn_w1", "L0_ffn_w2"]


def kernel(**inputs):
    import numpy as _np
    import concourse.bacc as _bacc
    from concourse.bass_utils import run_bass_kernel_spmd as _run

    nc = _bacc.Bacc("TRN2", target_bir_lowering=False, num_devices=1)
    arrays, args = {}, []
    for name in _INS:
        a = _np.ascontiguousarray(inputs[name])
        if a.ndim == 0:
            a = a.reshape(1)
        arrays[f"in_{name}"] = a
        args.append(nc.dram_tensor(f"in_{name}", a.shape, mybir.dt.from_np(a.dtype),
                                   kind="ExternalInput").ap())
    args.append(nc.dram_tensor("out_0", inputs["x"].shape, F32, kind="ExternalOutput").ap())
    build(nc, *args)
    r = _run(nc, [arrays], core_ids=[0])
    return r.results[0]["out_0"]
```

```python
from contextlib import ExitStack

import concourse.bass as bass
from concourse import mybir

F32 = mybir.dt.float32
F32R = mybir.dt.float32r
ALU = mybir.AluOpType
ACT = mybir.ActivationFunctionType
AX = mybir.AxisListType

P = 128
BANK = 512
TOPK = 8
EPS = 1e-5
NEG = -3.0e38

TIMETABLE = (
    [(0, s, j) for s, j in ((1, "v4"), (2, "v5"), (3, "q3"), (4, "k3.0"), (5, "k3.1"), (6, "xt0"),
                            (7, "xt1"), (9, "pa"), (11, "out0"), (11, "out1"), (15, "pc"),
                            (15, "pz"))]
    + [(1, s, j) for s, j in ((4, "mix0"), (4, "mix1"), (5, "ct0"), (5, "ct1"), (5, "ct2"),
                              (7, "ct3"), (8, "yt0"), (9, "yt1"), (11, "q0"), (13, "k0.0"),
                              (13, "k0.1"))]
    + [(2, s, j) for s, j in ((0, "rt0"), (1, "rt1"), (3, "gate"), (8, "q1"), (10, "k1.0"),
                              (11, "k1.1"), (13, "wt0"), (14, "wt1"))]
    + [(3, s, j) for s, j in ((1, "merge"), (4, "mt"), (5, "q2"), (7, "k2.0"), (9, "k2.1"),
                              (10, "v0"), (11, "v1"), (13, "v2"), (15, "v3"))]
)
NEXT = {"xt0", "xt1", "pa", "pc", "pz", "mix0", "mix1", "yt0", "yt1", "ct0", "ct1", "ct2", "ct3",
        "q0", "k0.0", "k0.1", "q1", "k1.0", "k1.1", "q2", "k2.0", "k2.1", "v0", "v1", "v2", "v3"}
PAST = {"out0", "out1", "rt0", "rt1", "gate", "wt0", "wt1", "merge", "mt"}
ORDER = [j for _, _, j in TIMETABLE]
STEPS = 16
UNIT_AT = 1
PV_AT = {6: 0, 10: 1}
LAST_PV_AT = 1
SUM_AT = {6: 0, 10: 1, 14: 2}
TURN_AT = 11
ROWS_AT = 14
LATE_AT = 2


MAXIMA = ((3, 0, 3, 0, 0, 2, 2, 1, 2, 2, 1),
          (0, 2, 1, 0, 2, 1, 3, 2, 2, 2, 1),
          (3, 2, 0, 0, 0, 2, 2, 2, 1, 2, 2),
          (1, 3, 1, 0, 2, 3, 0, 0, 2, 2, 2))


def maxima_at(kt, s):
    done = sum(MAXIMA[kt][:s])
    return range(done, done + sum(MAXIMA[kt][s:s + 1]))


def build(nc, x, ctx_in, aWq, aWk, aWo, U_b, V_b, W_b, bias_b, U_t, V_t, W_t, X_t, bias_t, alpha,
          xWq, xWkv, xWo, gate_w, gate_b, w1, w2, out):
    B, T, D = x.shape
    _, S, DC = ctx_in.shape
    R = V_b.shape[1]
    E, _, H = w1.shape
    NH = 16
    HD = D // NH
    SCALE = float(HD) ** -0.5
    KD, KC = D // P, DC // P
    TT = T // 2
    SK = 125
    NK = S // SK
    SC = (0, 376, S)
    G = KD
    LAST = B - 1
    assert T == 224 and NK * SK == S and R == P and G == 4 and 4 * HD == P and E == 32

    PRO = ["xt0", "xt1", "pa", "pc", "pz", "ct0", "ct1", "ct2", "ct3", "mix0", "mix1", "v0", "v1",
           "yt0", "yt1", "q0", "k0.0", "k0.1", "q1", "k1.0", "k1.1", "q2", "k2.0", "k2.1", "v2", "v3"]
    assert set(PRO) == NEXT and PRO[-2:] == ORDER[-2:]
    SEQ = {"pro": PRO, "first": [j for j in ORDER if j not in PAST], "mid": ORDER,
           "last": [j for j in ORDER if j not in NEXT], "tail": [j for j in ORDER if j in PAST]}
    N_PRO, N_FIRST, N_MID = len(PRO), len(SEQ["first"]), len(ORDER)
    BASE = {"pro": 0, "first": N_PRO, "mid": N_PRO + N_FIRST - N_MID,
            "last": N_PRO + N_FIRST - N_MID + N_MID * LAST}
    BASE["tail"] = BASE["last"] + len(SEQ["last"])
    assert N_MID % 2 == 0

    def place(job, kind):
        return BASE[kind] + SEQ[kind].index(job)

    def number(job, kind, b):
        n = place(job, kind)
        return b * N_MID + n if kind == "mid" else n

    def batch_of(job, kind, b):
        return b + 1 if job in NEXT else b - 1 if job in PAST else b

    def before(job, kind, b):
        n = SEQ[kind].index(job)
        if n >= 2:
            p = SEQ[kind][n - 2]
            return p, batch_of(p, kind, b)
        if kind == "pro":
            return None
        if kind == "tail":
            p = SEQ["last"][n - 2]
            return p, batch_of(p, "last", b - 1)
        return PRO[n - 2], b

    es = ExitStack()
    with es:
        def sem(name):
            return es.enter_context(nc.semaphore(name))

        def sb(stack, name, shape, dt=F32):
            return stack.enter_context(nc.sbuf_tensor(name, shape, dt))

        bank = [es.enter_context(nc.psum_tensor(f"bank{i}", [P, BANK], F32)) for i in range(8)]
        router = nc.dram_tensor("router", [B, 4, E, T], F32).ap()
        o_parts = nc.dram_tensor("o_parts", [B, 4, E, D], F32).ap()

        ident = sb(es, "ident", [P, P])
        merged_T = sb(es, "merged_T", [P, KD, E, B])
        b1_rows = sb(es, "b1_rows", [P, 4, P])
        b1_loaded = sem("b1_loaded")
        SLOTS = 8
        D1, H1 = KD * P, H
        HC = H // BANK
        HT = BANK // P

        chunk_in = [sem(f"chunk_in{i}") for i in range(SLOTS)]
        ones = sb(es, "ones", [P, T])
        halves = sb(es, "halves", [P, 2])
        eps_tile = sb(es, "eps_tile", [P, 2])
        relay = sb(es, "relay", [1, 8])
        bias_row = sb(es, "bias_row", [TT, D])
        wo_T = sb(es, "wo_T", [P, KD, D])
        gate_T = sb(es, "gate_T", [P, KD, E])
        gate_bias = sb(es, "gate_bias", [E, 1])

        home = ExitStack()
        filled = [0]
        top = nc.sbuf_bytes_remaining

        def inside(name, rows, shape, dt=F32):
            n = 4
            for d in shape:
                n *= d
            filled[0] += -(-n // 32) * 32
            return sb(home, name, [rows] + shape, dt)

        def end_slot():
            rest = -filled[0] % (8 * H) // 4
            if rest:
                inside(f"rest{filled[0] // (8 * H)}", P, [rest])

        in_q = inside("in_q", P, [KD, 2 * R])
        in_k = inside("in_k", P, [KD, 2 * R])
        in_z = inside("in_z", P, [KD, R])
        mix_out = inside("mix_out", P, [2, D])
        a_mix = inside("a_mix", P, [2, T])
        end_slot()
        inv_count = inside("inv_count", P, [T])
        wq_T = inside("wq_T", P, [KD, D])
        wk_T = inside("wk_T", P, [KC, D])
        c_mix = inside("c_mix", P, [2, T])
        end_slot()
        x_in = inside("x_in", TT, [2, D])
        ctx_nat = inside("ctx_nat", SK, [NK, DC])
        ctx_T = inside("ctx_T", P, [KC, S])
        end_slot()
        wv_T = inside("wv_T", P, [KC, D])
        yT = inside("yT", P, [KD, T])
        z_mix = inside("z_mix", P, [T])
        k_hi = inside("k_hi", P, [S], F32R)
        k_lo = inside("k_lo", P, [S], F32R)
        q_hi = inside("q_hi", P, [T], F32R)
        q_lo = inside("q_lo", P, [T], F32R)
        end_slot()

        x_loaded = sem("x_loaded")
        ctx_loaded = sem("ctx_loaded")

        with ExitStack() as st:
            n_aq = sb(st, "n_aq", [P, KD, D])
            n_ak = sb(st, "n_ak", [P, KD, D])
            n_ao = sb(st, "n_ao", [P, KD, D])
            n_xq = sb(st, "n_xq", [P, KD, D])
            n_xo = sb(st, "n_xo", [P, KD, D])
            n_kv = sb(st, "n_kv", [P, 2 * KD, DC])
            vv = sb(st, "vv", [P, KD, 2 * R])
            ww = sb(st, "ww", [P, KD, 2 * R])
            uu = sb(st, "uu", [P, 2, KD, R])
            ao_T = sb(st, "ao_T", [P, KD, D])
            n_gate = sb(st, "n_gate", [E, D])
            bcol = sb(st, "bcol", [P, 2, KD])
            bmix = sb(st, "bmix", [P, KD])
            bwide = sb(st, "bwide", [P, KD, TT])
            al = sb(st, "al", [P, 1])
            s_iz = sem("s_iz")
            s_id = sem("s_id")
            s_full = sem("s_full")
            s_out = sem("s_out")
            s_one = sem("s_one")
            s_cnt = sem("s_cnt")
            s_bias = sem("s_bias")

            def rows(w):
                return w.rearrange("(k p) n -> p k n", p=P)

            loads = [("xq", n_xq[:], rows(xWq)), ("ao", n_ao[:], rows(aWo)),
                     ("xo", n_xo[:], rows(xWo)), ("kv", n_kv[:], rows(xWkv)),
                     ("gate", n_gate[:], gate_w), ("aq", n_aq[:], rows(aWq)),
                     ("vb", vv[:, :, 0:R], rows(V_b)), ("vt", vv[:, :, R:2 * R], rows(V_t)),
                     ("ak", n_ak[:], rows(aWk)), ("wb", ww[:, :, 0:R], rows(W_b)),
                     ("wt", ww[:, :, R:2 * R], rows(W_t)), ("ub", uu[:, 0], rows(U_b)),
                     ("ut", uu[:, 1], rows(U_t)), ("xt", in_z[:], rows(X_t)),
                     ("gb", gate_bias[:], gate_b.rearrange("(p o) -> p o", o=1)),
                     ("bb", bcol[:, 0, :], bias_b.rearrange("(k p) -> p k", p=P)),
                     ("bt", bcol[:, 1, :], bias_t.rearrange("(k p) -> p k", p=P)),
                     ("al", al[:], alpha.to_broadcast((P, 1)))]
            loaded = {name: sem(f"loaded_{name}") for name, _, _ in loads}

            flips = []
            needs = {}
            for name, src, dst in (("xq", n_xq, wq_T), ("ao", n_ao, ao_T), ("xo", n_xo, wo_T)):
                needs[len(flips)] = name
                for i in range(KD):
                    flips.append([(src[:, o, i * P:(i + 1) * P], dst[:, i, :]) for o in range(KD)])
            needs[len(flips)] = "kv"
            for h, dst in ((0, wk_T), (1, wv_T)):
                for i in range(KC):
                    flips.append([(n_kv[:, h * KD + o, i * P:(i + 1) * P], dst[:, i, :])
                                  for o in range(KD)])
            NF = len(flips)
            N_SETUP = NF + 1 + 2 * KD + 2 + 1

            with nc.Block() as block:
                @block.sync
                def _(sp):
                    for name, dst, src in loads:
                        with nc.allow_non_contiguous_dma("bias columns"):
                            sp.dma_start(dst, src).then_inc(loaded[name], 16)
                    sp.dma_start(x_in[:], x[0, :, :].rearrange("(t p) d -> p t d", p=TT)
                                 ).then_inc(x_loaded, 16)
                    sp.dma_start(ctx_nat[:], ctx_in[0, :, :].rearrange("(k p) d -> p k d", p=SK)
                                 ).then_inc(ctx_loaded, 16)
                    for name in ("gb", "xt"):
                        sp.wait_ge(loaded[name], 16)

                @block.gpsimd
                def _(pool):
                    nc.gpsimd.memset(ident[:], 0.0).then_inc(s_iz, 1)
                    pool.wait_ge(s_iz, 1)
                    nc.gpsimd.affine_select(out=ident[:], in_=ident[:], compare_op=ALU.not_equal,
                                            fill=1.0, base=0, pattern=[[-1, P]],
                                            channel_multiplier=1).then_inc(s_id, 1)
                    nc.gpsimd.memset(halves[:], -0.5)
                    nc.gpsimd.memset(eps_tile[:], EPS)
                    nc.gpsimd.memset(relay[:], 0.0)

                @block.tensor
                def _(pe):
                    pe.wait_ge(s_id, 1)
                    n = 0
                    for group in flips:
                        if n in needs:
                            pe.wait_ge(loaded[needs[n]], 16)
                        if n >= 8:
                            pe.wait_ge(s_out, n - 7)
                        for o, (src, _) in enumerate(group):
                            last = nc.tensor.transpose(bank[n % 8][:, o * P:(o + 1) * P], src,
                                                       ident[:])
                        last.then_inc(s_full, 1)
                        n += 1
                    pe.wait_ge(s_out, n - 7)
                    pe.wait_ge(loaded["gate"], 16)
                    for kd in range(KD):
                        last = nc.tensor.transpose(bank[n % 8][:, kd * E:(kd + 1) * E],
                                                   n_gate[:, kd * P:(kd + 1) * P],
                                                   ident[0:E, 0:E])
                    last.then_inc(s_full, 1)
                    n += 1
                    for names, w, v in ((("aq", "vb", "vt"), n_aq, vv), (("ak", "wb", "wt"), n_ak, ww)):
                        for name in names:
                            pe.wait_ge(loaded[name], 16)
                        for m in range(KD):
                            pe.wait_ge(s_out, n - 7)
                            for k in range(KD):
                                last = nc.tensor.matmul(bank[n % 8][:, 0:2 * R],
                                                        w[:, k, m * P:(m + 1) * P], v[:, k, :],
                                                        start=(k == 0), stop=(k == KD - 1))
                            last.then_inc(s_full, 1)
                            n += 1
                    for g in range(2):
                        pe.wait_ge(loaded["ub" if g == 0 else "ut"], 16)
                        pe.wait_ge(s_out, n - 7)
                        for k in range(KD):
                            last = nc.tensor.matmul(bank[n % 8][:], uu[:, g, k, :], ao_T[:, k, :],
                                                    start=(k == 0), stop=(k == KD - 1))
                        last.then_inc(s_full, 1)
                        n += 1
                    pe.wait_ge(s_out, n - 7)
                    pe.wait_ge(s_bias, 3)
                    for k in range(KD):
                        last = nc.tensor.matmul(bank[n % 8][0:TT, :], bwide[:, k, :], ao_T[:, k, :],
                                                start=(k == 0), stop=(k == KD - 1))
                    last.then_inc(s_full, 1)
                    assert n + 1 == N_SETUP

                @block.scalar
                def _(act):
                    n = 0
                    for group in flips:
                        act.wait_ge(s_full, n + 1)
                        nc.scalar.copy(group[0][1], bank[n % 8][:]).then_inc(s_out, 1)
                        n += 1
                    act.wait_ge(s_full, n + 1)
                    nc.scalar.copy(gate_T[:].rearrange("p k e -> p (k e)"),
                                   bank[n % 8][:, 0:KD * E]).then_inc(s_out, 1)
                    n += 1
                    for dst in (in_q, in_k):
                        for m in range(KD):
                            act.wait_ge(s_full, n + 1)
                            nc.scalar.copy(dst[:, m, :], bank[n % 8][:, 0:2 * R]).then_inc(s_out, 1)
                            n += 1
                    act.wait_ge(s_full, n + 1)
                    nc.scalar.copy(mix_out[:, 0, :], bank[n % 8][:]).then_inc(s_out, 1)
                    n += 1
                    act.wait_ge(s_full, n + 1)
                    act.wait_ge(loaded["al"], 16)
                    nc.scalar.mul(mix_out[:, 1, :], bank[n % 8][:], al[:, 0:1]).then_inc(s_out, 1)
                    n += 1
                    act.wait_ge(s_full, n + 1)
                    nc.scalar.copy(bias_row[:], bank[n % 8][0:TT, :]).then_inc(s_out, 1)

                @block.vector
                def _(dve):
                    nc.vector.memset(ones[:], 1.0).then_inc(s_one, 1)
                    dve.wait_ge(s_one, 1)
                    nc.vector.tensor_tensor_scan(inv_count[:], ones[:], ones[:], 0.0, ALU.mult,
                                                 ALU.add).then_inc(s_cnt, 1)
                    dve.wait_ge(s_cnt, 1)
                    nc.vector.reciprocal(inv_count[:], inv_count[:]).then_inc(s_cnt, 1)
                    for name in ("bb", "bt", "al"):
                        dve.wait_ge(loaded[name], 16)
                    nc.vector.tensor_scalar(bmix[:], bcol[:, 1, :], al[:, 0:1], None,
                                            ALU.mult).then_inc(s_bias, 1)
                    dve.wait_ge(s_bias, 1)
                    nc.vector.tensor_tensor(bmix[:], bmix[:], bcol[:, 0, :],
                                            ALU.add).then_inc(s_bias, 1)
                    dve.wait_ge(s_bias, 2)
                    nc.vector.tensor_copy(bwide[:], bmix[:].unsqueeze(2).to_broadcast([P, KD, TT])
                                          ).then_inc(s_bias, 1)

        def load_chunk(sp, e, q, slot):
            if q < 2:
                src = w1[bass.ds(e, 1), q * 2 * P:(q + 1) * 2 * P, :].rearrange(
                    "o (k p) n -> p (o k) n", p=P)
                dst = ring[:, slot, :].rearrange("p (k n) -> p k n", k=2)
                sp.dma_start(dst, src).then_inc(chunk_in[slot], 16)
                return
            t0 = (q - 2) * 2
            src = w2[bass.ds(e, 1), 0:H1, :].rearrange(
                "o (c t p) n -> p (o c) t n", t=HT, p=P)[:, :, t0:t0 + 2, :]
            dst = ring[:, slot, :].rearrange("p (c t n) -> p c t n", c=HC, t=2)
            for c in range(HC):
                sp.dma_start(dst[:, c], src[:, c]).then_inc(chunk_in[slot], 16)

        k_st, q_st = [], []
        for i in range(G):
            k_st.append(inside(f"k_st{i}", 3 * HD + 2, [4, S], F32R))
            q_st.append(inside(f"q_st{i}", 3 * HD + 2, [4, T], F32R))
            if i == 2:
                max_lo = inside("max_lo", 8, [TT], F32R)
            if i == 3:
                max_hi = inside("max_hi", 8, [TT], F32R)
            end_slot()
        assert filled[0] == 8 * H * SLOTS and 0 <= top - nc.sbuf_bytes_remaining - filled[0] < 32
        home.close()
        ring = sb(es, "ring", [P, SLOTS, 2 * H])
        lay = ExitStack()

        x1 = sb(lay, "x1", [TT, 2, D])
        x1_kept = sb(lay, "x1_kept", [TT, 2, D])
        x2 = sb(lay, "x2", [TT, 2, D])
        xh = sb(lay, "xh", [TT, 2, D])
        xr = x2
        stats = sb(lay, "stats", [TT, 3, 2, 6])
        mean_var = sb(lay, "mean_var", [TT, 3, 2, 2])
        rstd = sb(lay, "rstd", [TT, 3, 2])
        xT = sb(lay, "xT", [P, KD, T])
        rT = xT
        g_mix = a_mix
        maxes = sb(lay, "maxes", [TT, 4, 2, 2])
        q_max = sb(lay, "q_max", [TT, 8])
        v = sb(lay, "v", [SK, NK, D])
        probs = [sb(lay, f"probs{i}", [SK, 4, 2 * T]) for i in range(2)]
        psum_keys = sb(lay, "psum_keys", [SK, 4, T])
        o_T = sb(lay, "o_T", [P, G, T])
        logits = sb(lay, "logits", [E, T])
        top8 = sb(lay, "top8", [E, 8])
        neg_top = sb(lay, "neg_top", [E, 1])
        beaten = sb(lay, "beaten", [E, T])
        chosen = beaten
        expo_sum = sb(lay, "expo_sum", [E, 1])
        inv_sum = sb(lay, "inv_sum", [E, 1])
        weight = sb(lay, "weight", [P, T])
        expo = weight[0:E, :]
        weight_T = sb(lay, "weight_T", [TT, 2, E])
        merged = sb(lay, "merged", [P, D])

        work_full = sem("work_full")
        xt_ready = sem("xt_ready")
        mixed = sem("mixed")
        scanned = sem("scanned")
        x1_ready = sem("x1_ready")
        yt_ready = sem("yt_ready")
        ctx_ready = sem("ctx_ready")
        q_hi_ready = sem("q_hi_ready")
        q_ready = sem("q_ready")
        k_hi_ready = sem("k_hi_ready")
        k_ready = sem("k_ready")
        v_ready = sem("v_ready")
        x2_ready = sem("x2_ready")
        rt_ready = sem("rt_ready")
        logits_ready = sem("logits_ready")
        wt_ready = sem("wt_ready")
        merged_ready = sem("merged_ready")
        mt_ready = sem("mt_ready")
        k_stacked = [sem(f"k_stacked{i}") for i in range(G)]
        q_stacked = [sem(f"q_stacked{i}") for i in range(G)]
        max_stacked = [sem(f"max_stacked{i}") for i in range(G)]
        s_full1 = sem("s_full1")
        s_drained = sem("s_drained")
        q_max_ready = sem("q_max_ready")
        max_hi_ready = sem("max_hi_ready")
        max_ready = sem("max_ready")
        scores_ready = sem("scores_ready")
        probs_ready = sem("probs_ready")
        pv_done = sem("pv_done")
        keys_summed = sem("keys_summed")
        pool_chain = sem("pool_chain")
        den_done = sem("den_done")
        inv_ready = sem("inv_ready")
        o_ready = sem("o_ready")
        stats_done = sem("stats_done")
        agg_done = sem("agg_done")
        eps_done = sem("eps_done")
        rstd_done = sem("rstd_done")
        xh_ready = sem("xh_ready")
        xr_ready = sem("xr_ready")
        x_bias_ready = sem("x_bias_ready")
        x1_kept_ready = sem("x1_kept_ready")
        x2_stored = sem("x2_stored")
        top8_ready = sem("top8_ready")
        neg_ready = sem("neg_ready")
        router_chain = sem("router_chain")
        expo_ready = sem("expo_ready")
        weight_ready = sem("weight_ready")
        router_stored = sem("router_stored")
        constants = sem("constants")

        OUT = {"xt0": (xt_ready, 2, 0), "xt1": (xt_ready, 2, 1), "pa": (scanned, 3, 0),
               "pc": (scanned, 3, 1), "pz": (scanned, 3, 2), "mix0": (x1_ready, 2, 0),
               "mix1": (x1_ready, 2, 1), "yt0": (yt_ready, 2, 0), "yt1": (yt_ready, 2, 1),
               "out0": (x2_ready, 2, 0), "out1": (x2_ready, 2, 1), "rt0": (rt_ready, 2, 0),
               "rt1": (rt_ready, 2, 1), "gate": (logits_ready, 1, 0), "wt0": (wt_ready, 2, 0),
               "wt1": (wt_ready, 2, 1), "merge": (merged_ready, 1, 0), "mt": (mt_ready, 1, 0)}
        for i in range(4):
            OUT[f"ct{i}"] = (ctx_ready, 4, i)
            OUT[f"q{i}"] = (q_ready, 4, i)
            for c in range(2):
                OUT[f"k{i}.{c}"] = (k_ready, 8, 2 * i + c)
        for i in range(NK):
            OUT[f"v{i}"] = (v_ready, NK, i)

        def wait_out(eng, job, b):
            s, per, i = OUT[job]
            eng.wait_ge(s, b * per + (i + 1))

        def group_before(b, kt):
            return (kt - 1, b + 1) if kt else (G - 1, b)

        def isint(b):
            return isinstance(b, int)

        def jobs_at(kind, kt, s):
            return [j for g, st_, j in TIMETABLE if (g, st_) == (kt, s) and j in SEQ[kind]]

        def bank_of(job, kind):
            return bank[place(job, kind) % 2]

        def norm_no(which, kind, b):
            if kind == "first":
                return 2 + {0: 0, 1: 1}[which]
            if kind == "mid":
                return b * 3 + {0: 1, 1: 2, 2: 3}[which]
            if kind == "last":
                return LAST * 3 + 1
            return 3 * B - 1

        def chunk(c):
            return slice(SC[c], SC[c + 1])

        def batches(eng, step):
            step("pro", -1)
            step("first", 0)
            with eng.Fori(1, LAST) as b:
                step("mid", b)
            step("last", LAST)
            step("tail", LAST + 1)

        with nc.Block() as block:
            @block.sync
            def _(sp):
                def value(x):
                    return x if isint(x) else sp.snap(x)

                def load_x(b):
                    b = value(b)
                    sp.wait_ge(x1_ready, b * 2)
                    sp.dma_start(x_in[:], x[b, :, :].rearrange("(t p) d -> p t d", p=TT)
                                 if isint(b) else x[bass.ds(b, 1), :, :].rearrange(
                                     "o (t p) d -> p (o t) d", p=TT)).then_inc(x_loaded, 16)

                def load_ctx(b):
                    b = value(b)
                    sp.wait_ge(ctx_ready, b * 4)
                    sp.dma_start(ctx_nat[:], ctx_in[b, :, :].rearrange("(k p) d -> p k d", p=SK)
                                 if isint(b) else ctx_in[bass.ds(b, 1), :, :].rearrange(
                                     "o (k p) d -> p (o k) d", p=SK)).then_inc(ctx_loaded, 16)

                def stack(b, kt):
                    slot = kt
                    q_count = value(b * 4 + (kt + 1))
                    k_count = value(b * 8 + 2 * (kt + 1))
                    sp.wait_ge(q_ready, q_count)
                    for j in range(4):
                        src = slice(j * HD, (j + 1) * HD)
                        for r, part in enumerate((q_hi, q_hi, q_lo)):
                            sp.dma_start(q_st[slot][r * HD:(r + 1) * HD, j, :].bitcast(F32),
                                         part[src, :].bitcast(F32)).then_inc(q_stacked[slot], 16)
                    sp.wait_ge(k_ready, k_count)
                    for j in range(4):
                        src = slice(j * HD, (j + 1) * HD)
                        for r, part in enumerate((k_hi, k_lo, k_hi)):
                            sp.dma_start(k_st[slot][r * HD:(r + 1) * HD, j, :].bitcast(F32),
                                         part[src, :].bitcast(F32)).then_inc(k_stacked[slot], 16)

                def store(b):
                    sp.wait_ge(x2_ready, b * 2 + 2)
                    dst = out[b, :, :].rearrange("(t p) d -> p t d", p=TT) if isint(b) else \
                        out[bass.ds(b, 1), :, :].rearrange("o (t p) d -> p (o t) d", p=TT)
                    sp.dma_start(dst, x2[:]).then_inc(x2_stored, 16)

                def keep_weight(b):
                    sp.wait_ge(weight_ready, b + 1)
                    sp.dma_start(router[bass.ds(b, 1), :, :, :].rearrange("o c e t -> e (o c) t"),
                                 weight[0:E, :].unsqueeze(1).to_broadcast([E, 4, T])
                                 ).then_inc(router_stored, 16)

                def first_weights(slots):
                    for slot in slots:
                        load_chunk(sp, slot // 4, slot % 4, slot)

                def expert_biases():
                    QB = HC * HT
                    per = P // QB
                    for e in range(E):
                        r = e % per * QB
                        sp.dma_start(b1_rows[r:r + QB, e // per, :],
                                     w1[e, D1, :].rearrange("(q n) -> q n", n=P)
                                     ).then_inc(b1_loaded, 16)

                def step(kind, b):
                    if kind == "pro":
                        stack(0, 0)
                        stack(0, 1)
                        stack(0, 2)
                        return
                    if kind == "tail":
                        sp.wait_ge(scores_ready, (LAST * 4 + 3) * 12 + 1)
                        first_weights([6])
                        sp.wait_ge(scores_ready, (LAST * 4 + 4) * 12)
                        first_weights([7])
                        store(b - 1)
                        keep_weight(b - 1)
                        return
                    if kind != "last":
                        load_x(b + 1)
                    for kt in range(4):
                        if kt == 1 and kind != "first":
                            store(b - 1)
                        if kt == 0:
                            stack(b, 3)
                        elif kind != "last":
                            stack(b + 1, kt - 1)
                        if kt == 0 and kind != "last":
                            load_ctx(b + 1)
                        if kt == 3 and kind != "first":
                            keep_weight(b - 1)
                        if kind == "last" and kt == 1:
                            expert_biases()
                            sp.wait_ge(x1_ready, 2 * B)
                            first_weights([0])
                            sp.wait_ge(v_ready, NK * B)
                            sp.wait_ge(q_ready, 4 * B)
                            sp.wait_ge(k_ready, 8 * B)
                            first_weights([1, 2])
                            sp.wait_ge(q_stacked[3], 192 * B)
                            sp.wait_ge(k_stacked[3], 192 * B)
                            first_weights([3])
                        if kind == "last" and kt >= 2:
                            sp.wait_ge(scores_ready, (LAST * 4 + kt - 1) * 12)
                            first_weights([2 + kt])

                batches(sp, step)
                sp.wait_ge(x2_stored, 16 * B)
                sp.wait_ge(router_stored, 16 * B)

            @block.gpsimd
            def _(pool):
                def fill_constants():
                    pool.drain()
                    nc.gpsimd.memset(weight[:], 0.0).then_inc(constants, 1)
                    nc.gpsimd.memset(merged[:], 0.0).then_inc(constants, 1)
                    pool.wait_ge(constants, 2)
                    for i in range(G):
                        nc.gpsimd.memset(k_st[i][3 * HD:3 * HD + 2, :, :].bitcast(F32), 1.0
                                         ).then_inc(constants, 1)
                    pool.wait_ge(constants, 6)

                def root(which, n):
                    pool.drain()
                    pool.wait_ge(agg_done, n * 2 + 2)
                    nc.gpsimd.tensor_tensor(rstd[:, which, :], mean_var[:, which, :, 1],
                                            eps_tile[0:TT, :], ALU.add).then_inc(eps_done, 1)
                    pool.wait_ge(eps_done, n + 1)
                    nc.gpsimd.tensor_tensor(rstd[:, which, :], rstd[:, which, :],
                                            halves[0:TT, :], ALU.pow).then_inc(rstd_done, 1)

                def bias(b):
                    pool.drain()
                    pool.wait_ge(xh_ready, b * 4 + 2)
                    nc.gpsimd.tensor_tensor(x_in[:], x_in[:],
                                            bias_row[:].unsqueeze(1).to_broadcast([TT, 2, D]),
                                            ALU.add).then_inc(x_bias_ready, 1)

                def keep(b):
                    pool.drain()
                    pool.wait_ge(x1_ready, b * 2 + 2)
                    if not (isint(b) and b == 0):
                        pool.wait_ge(x2_ready, b * 2)
                    nc.gpsimd.tensor_tensor(
                        x1_kept[:], x1[:], ones[0:TT, 0:1].unsqueeze(2).to_broadcast([TT, 2, D]),
                        ALU.mult).then_inc(x1_kept_ready, 1)

                def sum_keys(b, kt, c):
                    p = probs[(3 * kt + c) % 2]
                    pool.drain()
                    pool.wait_ge(probs_ready, (b * 4 + kt) * 12 + (4 * c + 4))
                    lo, hi = p[:, :, 0:T], p[:, :, T:2 * T]
                    if c == 0:
                        if not (isint(b) and b == 0 and kt == 0):
                            pool.wait_ge(den_done, b * 4 + kt)
                        nc.gpsimd.tensor_tensor(psum_keys[:], lo, hi, ALU.add
                                                ).then_inc(keys_summed, 1)
                        return
                    pool.wait_ge(keys_summed, (b * 4 + kt) * 3 + c)
                    nc.gpsimd.tensor_tensor(psum_keys[:], psum_keys[:], lo, ALU.add
                                            ).then_inc(pool_chain, 1)
                    pool.wait_ge(pool_chain, (b * 4 + kt) * 2 + c)
                    nc.gpsimd.tensor_tensor(psum_keys[:], psum_keys[:], hi, ALU.add
                                            ).then_inc(keys_summed, 1)

                def step(kind, b):
                    if kind == "pro":
                        root(0, 0)
                        bias(0)
                        root(1, 1)
                        fill_constants()
                        return
                    if kind == "tail":
                        root(2, 3 * B - 1)
                        return
                    for kt in range(4):
                        for s in range(STEPS):
                            if (kt, s) == (1, 0):
                                keep(b)
                            if (kt, s) == (0, 3) and kind != "last":
                                root(0, norm_no(0, kind, b))
                            if (kt, s) == (0, 5) and kind != "last":
                                bias(b + 1)
                            if (kt, s) == (1, 5) and kind != "last":
                                root(1, norm_no(1, kind, b))
                            if (kt, s) == (1, 11) and kind != "first":
                                root(2, norm_no(2, kind, b))
                            if s in SUM_AT:
                                sum_keys(b, kt, SUM_AT[s])

                batches(pool, step)

            @block.scalar
            def _(act):
                def fill(job, kind, b):
                    bb = batch_of(job, kind, b)
                    ps = bank_of(job, kind)
                    s, per, i = OUT[job]
                    full = number(job, kind, b) + 1
                    if job[:2] in ("xt", "yt", "rt"):
                        dst = {"xt": xT, "yt": yT, "rt": rT}[job[:2]]
                        act.wait_ge(work_full, full)
                        nc.scalar.copy(dst[:, 2 * i:2 * i + 2, :].rearrange("p k n -> p (k n)"),
                                       ps[:, 0:2 * T]).then_inc(s, 1)
                    elif job[:2] == "ct":
                        kc, half = i % 2, i // 2
                        act.wait_ge(work_full, full)
                        nc.scalar.copy(ctx_T[:, kc, half * 3 * SK:(half + 1) * 3 * SK],
                                       ps[:, 0:3 * SK]).then_inc(s, 1)
                    elif job[0] == "q":
                        if not (isint(bb) and bb == 0 and i == 0):
                            slot, n = group_before(bb, i)
                            act.wait_ge(q_stacked[slot], n * 192)
                        act.wait_ge(work_full, full)
                        nc.scalar.copy(q_hi[:], ps[:, 0:T]).then_inc(q_hi_ready, 1)
                    elif job[0] == "k":
                        kt, c = i // 2, i % 2
                        if c == 0 and not (isint(bb) and bb == 0 and kt == 0):
                            slot, n = group_before(bb, kt)
                            act.wait_ge(k_stacked[slot], n * 192)
                        act.wait_ge(work_full, full)
                        nc.scalar.copy(k_hi[:, chunk(c)], ps[:, 0:SC[c + 1] - SC[c]]
                                       ).then_inc(k_hi_ready, 1)
                    elif job[0] == "v":
                        act.wait_ge(work_full, full)
                        nc.scalar.copy(v[:, i, :], ps[0:SK, :]).then_inc(s, 1)
                    elif job == "gate":
                        act.wait_ge(work_full, full)
                        nc.scalar.activation(logits[:], ps[0:E, 0:T], ACT.Identity,
                                             bias=gate_bias[:, 0:1]).then_inc(s, 1)
                    elif job[:2] == "wt":
                        act.wait_ge(work_full, full)
                        nc.scalar.copy(weight_T[:, i, :], ps[0:TT, 0:E]).then_inc(s, 1)
                    elif job == "merge":
                        if isint(bb) or kind == "mid":
                            act.wait_ge(constants, 4)
                        act.wait_ge(work_full, full)
                        nc.scalar.copy(merged[0:E, :], ps[0:E, :]).then_inc(s, 1)

                def router_exp(b):
                    if isint(b) and b == 0:
                        act.wait_ge(constants, 4)
                    else:
                        act.wait_ge(router_stored, b * 16)
                    act.wait_ge(neg_ready, b + 1)
                    nc.scalar.activation(expo[:], logits[:], ACT.Exp, bias=neg_top[:, 0:1],
                                         accum_out=expo_sum[:]).then_inc(expo_ready, 1)

                def exp(b, kt, u):
                    c, j = u // 4, u % 4
                    n = 3 * kt + c
                    if not (isint(b) and b == 0 and n < 2):
                        act.wait_ge(pv_done, b * 12 + (n - 1))
                        act.wait_ge(keys_summed, b * 12 + (n - 1))
                    act.wait_ge(scores_ready, (b * 4 + kt) * 12 + (u + 1))
                    nc.scalar.activation(probs[n % 2][:, j, :], bank[5 + u % 2][0:SK, 0:2 * T],
                                         ACT.Exp, scale=SCALE).then_inc(probs_ready, 1)

                def stack_max(b, kt):
                    slot = kt
                    act.wait_ge(max_ready, b * 4 + (kt + 1))
                    for r, part in enumerate((max_hi, max_lo)):
                        row = 3 * HD + r
                        act.dma_start(q_st[slot][row:row + 1, :, :].rearrange(
                            "o j (t n) -> o (j t) n", t=2).bitcast(F32), part[:, :].bitcast(F32)
                                     ).then_inc(max_stacked[slot], 16)

                def step(kind, b):
                    if kind in ("pro", "tail"):
                        for job in SEQ[kind]:
                            fill(job, kind, b)
                            if job == "gate":
                                router_exp(b - 1)
                            if job == "k1.1":
                                stack_max(0, 0)
                        return
                    for kt in range(4):
                        for s in range(STEPS):
                            for job in jobs_at(kind, kt, s):
                                fill(job, kind, b)
                            if (kt, s) == (2, 6) and kind != "first":
                                router_exp(b - 1)
                            if 0 <= s - UNIT_AT < 12:
                                exp(b, kt, s - UNIT_AT)
                            if s == ROWS_AT and kt < 3:
                                stack_max(b, kt + 1)
                            elif s == ROWS_AT and kind != "last":
                                stack_max(b + 1, 0)

                batches(act, step)

            @block.vector
            def _(dve):

                def relay_wait(b, place):
                    if not isint(b):
                        nc.vector.tensor_copy(relay[0:1, place + 1:place + 2], relay[0:1, 0:1])

                def norm_stats(which, n, src):
                    for t in range(2):
                        nc.vector.bn_stats(stats[:, which, t, :], src[:, t, :]
                                           ).then_inc(stats_done, 1)
                    for t in range(2):
                        dve.wait_ge(stats_done, n * 2 + (t + 1))
                        relay_wait(n, which * 2 + t)
                        nc.vector.bn_aggr(mean_var[:, which, t, :], stats[:, which, t, :]
                                          ).then_inc(agg_done, 1)

                def norm_apply(which, n, src, dst, s):
                    dve.wait_ge(rstd_done, n + 1)
                    for t in range(2):
                        nc.vector.tensor_scalar(dst[:, t, :], src[:, t, :],
                                                mean_var[:, which, t, 0:1],
                                                rstd[:, which, t:t + 1],
                                                ALU.subtract, ALU.mult).then_inc(s, 1)

                def mixer_stats(b, n):
                    dve.wait_ge(x_loaded, b * 16 + 16)
                    norm_stats(0, n, x_in)

                def mixer_apply(b, n):
                    if not (isint(b) and b == 0):
                        dve.wait_ge(yt_ready, b * 2)
                    norm_apply(0, n, x_in, xh, xh_ready)

                def attention_stats(b, n):
                    dve.wait_ge(x1_ready, b * 2 + 2)
                    norm_stats(1, n, x1)

                def attention_apply(b, n):
                    dve.wait_ge(xt_ready, b * 2 + 2)
                    norm_apply(1, n, x1, xh, xh_ready)

                def router_stats(b, n):
                    dve.wait_ge(x2_ready, b * 2 + 2)
                    norm_stats(2, n, x2)

                def router_apply(b, n):
                    dve.wait_ge(x2_stored, b * 16 + 16)
                    norm_apply(2, n, x2, xr, xr_ready)

                def fill(job, kind, b):
                    bb = batch_of(job, kind, b)
                    ps = bank_of(job, kind)
                    s, per, i = OUT[job]
                    full = number(job, kind, b) + 1
                    if job == "pa":
                        dve.wait_ge(work_full, full)
                        nc.vector.tensor_tensor(
                            a_mix[:], ps[:, 0:2 * T].rearrange("p (g n) -> p g n", g=2),
                            inv_count[:].unsqueeze(1).to_broadcast([P, 2, T]), ALU.mult
                        ).then_inc(s, 1)
                    elif job == "pc":
                        dve.wait_ge(work_full, full)
                        nc.vector.tensor_tensor_scan(c_mix[:, 0, :], ones[:], ps[:, 0:T], 0.0,
                                                     ALU.mult, ALU.add).then_inc(mixed, 1)
                        nc.vector.tensor_tensor_scan(c_mix[:, 1, :], ones[:], ps[:, T:2 * T], 0.0,
                                                     ALU.mult, ALU.add).then_inc(s, 1)
                    elif job == "pz":
                        dve.wait_ge(work_full, full)
                        nc.vector.tensor_tensor_scan(z_mix[:], ones[:], ps[:, 0:T], 0.0,
                                                     ALU.mult, ALU.add).then_inc(s, 1)
                        dve.wait_ge(scanned, bb * 3 + 2)
                        dve.wait_ge(mixed, bb * 4 + 1)
                        nc.vector.tensor_tensor(g_mix[:], a_mix[:], c_mix[:], ALU.mult
                                                ).then_inc(mixed, 1)
                        dve.wait_ge(scanned, bb * 3 + 3)
                        nc.vector.tensor_tensor(z_mix[:], z_mix[:], inv_count[:], ALU.mult
                                                ).then_inc(mixed, 1)
                        dve.wait_ge(mixed, bb * 4 + 3)
                        nc.vector.tensor_tensor(g_mix[:, 1, :], g_mix[:, 1, :], z_mix[:],
                                                ALU.mult).then_inc(mixed, 1)
                    elif job[:3] == "mix":
                        if i == 0:
                            dve.wait_ge(x_bias_ready, bb + 1)
                            if not (isint(bb) and bb == 0):
                                dve.wait_ge(x1_kept_ready, bb)
                        dve.wait_ge(work_full, full)
                        nc.vector.tensor_tensor(x1[:, i, :], ps[0:TT, :], x_in[:, i, :],
                                                ALU.add).then_inc(s, 1)
                    elif job[0] == "q":
                        dve.wait_ge(work_full, full)
                        dve.wait_ge(q_hi_ready, bb * 4 + (i + 1))
                        nc.vector.tensor_tensor(q_lo[:], ps[:, 0:T], q_hi[:].bitcast(F32),
                                                ALU.subtract).then_inc(s, 1)
                    elif job[0] == "k":
                        c = i % 2
                        dve.wait_ge(work_full, full)
                        dve.wait_ge(k_hi_ready, bb * 8 + (i + 1))
                        nc.vector.tensor_tensor(k_lo[:, chunk(c)], ps[:, 0:SC[c + 1] - SC[c]],
                                                k_hi[:, chunk(c)].bitcast(F32), ALU.subtract
                                                ).then_inc(s, 1)
                    elif job[:3] == "out":
                        if i == 0:
                            dve.wait_ge(x1_kept_ready, bb + 1)
                            if not (isint(bb) and bb == 0):
                                dve.wait_ge(x2_stored, bb * 16)
                        dve.wait_ge(work_full, full)
                        nc.vector.tensor_tensor(x2[:, i, :], ps[0:TT, :], x1_kept[:, i, :],
                                                ALU.add).then_inc(s, 1)
                    elif job == "mt":
                        dve.wait_ge(work_full, full)
                        nc.vector.tensor_copy(
                            merged_T[:, :, :, bass.ds(bb, 1)],
                            ps[:].rearrange("p (k e o) -> p k e o", k=KD, o=1)[:, :, 0:E, :]
                        ).then_inc(s, 1)

                def router_top(b):
                    dve.wait_ge(logits_ready, b + 1)
                    relay_wait(b, 6)
                    nc.vector.max(top8[:], logits[:]).then_inc(top8_ready, 1)
                    dve.wait_ge(top8_ready, b + 1)
                    nc.vector.tensor_scalar(neg_top[:], top8[:, 0:1], -1.0, None, ALU.mult
                                            ).then_inc(neg_ready, 1)
                    nc.vector.match_replace(beaten[:], top8[:], logits[:], NEG
                                            ).then_inc(router_chain, 1)
                    dve.wait_ge(router_chain, b * 3 + 1)
                    nc.vector.tensor_tensor(chosen[:], logits[:], beaten[:], ALU.not_equal
                                            ).then_inc(router_chain, 1)

                def router_weight(b):
                    dve.wait_ge(expo_ready, b + 1)
                    nc.vector.reciprocal(inv_sum[:], expo_sum[:]).then_inc(router_chain, 1)
                    dve.wait_ge(router_chain, b * 3 + 3)
                    nc.vector.scalar_tensor_tensor(out=weight[0:E, :], in0=expo[:],
                                                   scalar=inv_sum[:, 0:1], in1=chosen[:],
                                                   op0=ALU.mult, op1=ALU.mult
                                                   ).then_inc(weight_ready, 1)

                def take_max(b, kt, n):
                    j, t, c = n // 4, n // 2 % 2, n % 2
                    g17 = (b * 4 + kt) * 17
                    dve.wait_ge(s_full1, g17 + (n + 1))
                    nc.vector.tensor_reduce(maxes[:, j, t, c:c + 1],
                                            bank[2 + n % 3][0:TT, 0:SC[c + 1] - SC[c]], AX.X,
                                            ALU.max).then_inc(s_drained, 1)

                def join_maxima(b, kt):
                    g = b * 4 + kt
                    dve.wait_ge(s_drained, g * 16 + 16)
                    nc.vector.tensor_reduce(q_max[:], maxes[:].rearrange("p j t c -> p (j t) c"),
                                            AX.X, ALU.max).then_inc(q_max_ready, 1)

                def max_rows(b, kt):
                    g = b * 4 + kt
                    dve.wait_ge(s_full1, g * 17 + 17)
                    if not (isint(b) and b == 0 and kt == 0):
                        slot, n = group_before(b, kt)
                        dve.wait_ge(max_stacked[slot], n * 32)
                    nc.vector.tensor_scalar(max_hi[:], bank[2][0:8, 0:TT], -1.0, None, ALU.mult
                                            ).then_inc(max_hi_ready, 1)
                    dve.wait_ge(max_hi_ready, g + 1)
                    nc.vector.scalar_tensor_tensor(out=max_lo[:], in0=bank[2][0:8, 0:TT],
                                                   scalar=-1.0, in1=max_hi[:].bitcast(F32),
                                                   op0=ALU.mult, op1=ALU.subtract
                                                   ).then_inc(max_ready, 1)

                def normalise(b, kt):
                    g = b * 4 + kt
                    dve.wait_ge(den_done, g + 1)
                    nc.vector.reciprocal(o_T[:, kt, :], bank[7][:, T:2 * T]).then_inc(inv_ready, 1)
                    dve.wait_ge(inv_ready, g + 1)
                    nc.vector.tensor_tensor(o_T[:, kt, :], bank[7][:, 0:T], o_T[:, kt, :], ALU.mult
                                            ).then_inc(o_ready, 1)

                def step(kind, b):
                    if kind == "pro":
                        mixer_stats(0, 0)
                        mixer_apply(0, 0)
                        for job in SEQ[kind]:
                            fill(job, kind, b)
                            if job == "mix1":
                                attention_stats(0, 1)
                                attention_apply(0, 1)
                            if job == "k1.1":
                                for n in range(16):
                                    take_max(0, 0, n)
                                join_maxima(0, 0)
                                max_rows(0, 0)
                        return
                    if kind == "tail":
                        normalise(b - 1, G - 1)
                        for job in SEQ[kind]:
                            fill(job, kind, b)
                            if job == "out1":
                                router_stats(b - 1, norm_no(2, kind, b))
                                router_apply(b - 1, norm_no(2, kind, b))
                            if job == "gate":
                                router_top(b - 1)
                                router_weight(b - 1)
                        return
                    for kt in range(4):
                        nb, nk = (b, kt + 1) if kt < 3 else (b + 1, 0)
                        more = not (kt == 3 and kind == "last")
                        for s in range(STEPS):
                            if more and s == TURN_AT:
                                join_maxima(nb, nk)
                            if more and s == TURN_AT + 1:
                                max_rows(nb, nk)
                            if more:
                                for n in maxima_at(kt, s)[:1]:
                                    take_max(nb, nk, n)
                            for job in jobs_at(kind, kt, s):
                                fill(job, kind, b)
                            if more:
                                for n in maxima_at(kt, s)[1:]:
                                    take_max(nb, nk, n)
                            if kt == 0 and kind != "last":
                                if s == 2:
                                    mixer_stats(b + 1, norm_no(0, kind, b))
                                if s == 4:
                                    mixer_apply(b + 1, norm_no(0, kind, b))
                            if kind != "last":
                                if (kt, s) == (1, 4):
                                    attention_stats(b + 1, norm_no(1, kind, b))
                                if (kt, s) == (1, 6):
                                    attention_apply(b + 1, norm_no(1, kind, b))
                            if kt == 1 and kind != "first":
                                if s == 10:
                                    router_stats(b - 1, norm_no(2, kind, b))
                                if s == 12:
                                    router_apply(b - 1, norm_no(2, kind, b))
                            if kind != "first":
                                if (kt, s) == (2, 4):
                                    router_top(b - 1)
                                if (kt, s) == (2, 8):
                                    router_weight(b - 1)
                            if s == LATE_AT + 1:
                                if kt:
                                    normalise(b, kt - 1)
                                elif kind != "first":
                                    normalise(b - 1, G - 1)

                batches(dve, step)

            @block.tensor
            def _(pe):

                def fill(job, kind, b):
                    bb = batch_of(job, kind, b)
                    ps = bank_of(job, kind)
                    s, per, i = OUT[job]
                    prev = before(job, kind, b)
                    if prev:
                        wait_out(pe, *prev)
                    if job[:2] in ("xt", "yt", "rt"):
                        src = xr if job[0] == "r" else xh
                        if job[:2] == "xt":
                            pe.wait_ge(xh_ready, bb * 4 + 2)
                        elif job[:2] == "yt":
                            pe.wait_ge(xh_ready, bb * 4 + 4)
                        else:
                            pe.wait_ge(xr_ready, bb * 2 + 2)
                        for kk in range(2):
                            for t in range(2):
                                kd = 2 * i + kk
                                last = nc.tensor.transpose(
                                    ps[:, kk * T + t * TT:kk * T + (t + 1) * TT],
                                    src[:, t, kd * P:(kd + 1) * P], ident[0:TT, 0:TT])
                    elif job[:2] == "ct":
                        kc, half = i % 2, i // 2
                        pe.wait_ge(ctx_loaded, bb * 16 + 16)
                        for k in range(3):
                            last = nc.tensor.transpose(
                                ps[:, k * SK:(k + 1) * SK],
                                ctx_nat[:, half * 3 + k, kc * P:(kc + 1) * P], ident[0:SK, 0:SK])
                    elif job in ("pa", "pc", "pz"):
                        w = {"pa": in_q, "pc": in_k, "pz": in_z}[job]
                        pe.wait_ge(xt_ready, bb * 2 + 2)
                        for g in range(1 if job == "pz" else 2):
                            for kd in range(KD):
                                last = nc.tensor.matmul(ps[:, g * T:(g + 1) * T],
                                                        w[:, kd, g * R:(g + 1) * R], xT[:, kd, :],
                                                        start=(kd == 0), stop=(kd == KD - 1))
                    elif job[:3] == "mix":
                        pe.wait_ge(mixed, bb * 4 + 4)
                        for g in range(2):
                            last = nc.tensor.matmul(ps[0:TT, :], g_mix[:, g, i * TT:(i + 1) * TT],
                                                    mix_out[:, g, :], start=(g == 0), stop=(g == 1))
                    elif job[0] == "q":
                        pe.wait_ge(yt_ready, bb * 2 + 2)
                        for kd in range(KD):
                            last = nc.tensor.matmul(ps[:, 0:T], wq_T[:, kd, i * P:(i + 1) * P],
                                                    yT[:, kd, :], start=(kd == 0),
                                                    stop=(kd == KD - 1))
                    elif job[0] == "k":
                        kt, c = i // 2, i % 2
                        pe.wait_ge(ctx_ready, bb * 4 + 4)
                        for kc in range(KC):
                            last = nc.tensor.matmul(ps[:, 0:SC[c + 1] - SC[c]],
                                                    wk_T[:, kc, kt * P:(kt + 1) * P],
                                                    ctx_T[:, kc, chunk(c)], start=(kc == 0),
                                                    stop=(kc == KC - 1))
                    elif job[0] == "v":
                        pe.wait_ge(ctx_ready, bb * 4 + 4)
                        for kc in range(KC):
                            last = nc.tensor.matmul(ps[0:SK, :], ctx_T[:, kc, i * SK:(i + 1) * SK],
                                                    wv_T[:, kc, :], start=(kc == 0),
                                                    stop=(kc == KC - 1))
                    elif job[:3] == "out":
                        pe.wait_ge(o_ready, bb * 4 + 4)
                        for kt in range(G):
                            last = nc.tensor.matmul(ps[0:TT, :], o_T[:, kt, i * TT:(i + 1) * TT],
                                                    wo_T[:, kt, :], start=(kt == 0),
                                                    stop=(kt == G - 1))
                    elif job == "gate":
                        pe.wait_ge(rt_ready, bb * 2 + 2)
                        for kd in range(KD):
                            last = nc.tensor.matmul(ps[0:E, 0:T], gate_T[:, kd, :], rT[:, kd, :],
                                                    start=(kd == 0), stop=(kd == KD - 1))
                    elif job[:2] == "wt":
                        pe.wait_ge(weight_ready, bb + 1)
                        last = nc.tensor.transpose(ps[0:TT, 0:P], weight[:, i * TT:(i + 1) * TT],
                                                   ident[:])
                    elif job == "merge":
                        pe.wait_ge(wt_ready, bb * 2 + 2)
                        for t in range(2):
                            last = nc.tensor.matmul(ps[0:E, :], weight_T[:, t, :], xr[:, t, :],
                                                    start=(t == 0), stop=(t == 1))
                    elif job == "mt":
                        pe.wait_ge(merged_ready, bb + 1)
                        for kd in range(KD):
                            last = nc.tensor.transpose(ps[:, kd * P:(kd + 1) * P],
                                                       merged[:, kd * P:(kd + 1) * P],
                                                       ident[:])
                    last.then_inc(work_full, 1)

                def scores(b, kt, n):
                    j, t, c = n // 4, n // 2 % 2, n % 2
                    slot = kt
                    if n == 0:
                        pe.wait_ge(q_stacked[slot], b * 192 + 192)
                        pe.wait_ge(k_stacked[slot], b * 192 + 192)
                        if not (isint(b) and b == 0 and kt == 0):
                            pe.wait_ge(max_ready, b * 4 + kt)
                    elif n >= 3:
                        pe.wait_ge(s_drained, (b * 4 + kt) * 16 + (n - 2))
                    nc.tensor.matmul(bank[2 + n % 3][0:TT, 0:SC[c + 1] - SC[c]],
                                     q_st[slot][0:3 * HD, j, t * TT:(t + 1) * TT],
                                     k_st[slot][0:3 * HD, j, chunk(c)],
                                     start=True, stop=True).then_inc(s_full1, 1)

                def turn_max(b, kt):
                    pe.wait_ge(q_max_ready, b * 4 + (kt + 1))
                    nc.tensor.transpose(bank[2][0:8, 0:TT], q_max[:], ident[0:TT, 0:TT]
                                        ).then_inc(s_full1, 1)

                def scores_T(b, kt, u):
                    c, j = u // 4, u % 4
                    slot = kt
                    if u == 0:
                        pe.wait_ge(max_stacked[slot], b * 32 + 32)
                        if isint(b) and b == 0:
                            pe.wait_ge(constants, 6)
                    if not (isint(b) and b == 0 and kt == 0 and u < 2):
                        pe.wait_ge(probs_ready, (b * 4 + kt) * 12 + (u - 1))
                    for kk in range(2):
                        k = 2 * c + kk
                        last = nc.tensor.matmul(bank[5 + u % 2][0:SK, kk * T:(kk + 1) * T],
                                                k_st[slot][:, j, k * SK:(k + 1) * SK],
                                                q_st[slot][:, j, :], start=True, stop=True)
                    last.then_inc(scores_ready, 1)

                def values(b, kt, c):
                    p = probs[(3 * kt + c) % 2]
                    if c == 0:
                        if not (isint(b) and b == 0 and kt == 0):
                            pe.wait_ge(o_ready, b * 4 + kt)
                    if kt == 0:
                        pe.wait_ge(v_ready, b * NK + 2 * (c + 1))
                    pe.wait_ge(probs_ready, (b * 4 + kt) * 12 + (4 * c + 4))
                    for kk in range(2):
                        for j in range(4):
                            col = kt * P + j * HD
                            last = nc.tensor.matmul(bank[7][j * HD:(j + 1) * HD, 0:T],
                                                    v[:, 2 * c + kk, col:col + HD],
                                                    p[:, j, kk * T:(kk + 1) * T],
                                                    start=(c == 0 and kk == 0),
                                                    stop=(c == 2 and kk == 1))
                    last.then_inc(pv_done, 1)

                def denominators(b, kt):
                    pe.wait_ge(keys_summed, (b * 4 + kt) * 3 + 3)
                    for j in range(4):
                        last = nc.tensor.matmul(bank[7][j * HD:(j + 1) * HD, T:2 * T],
                                                ones[0:SK, 0:HD], psum_keys[:, j, :],
                                                start=True, stop=True)
                    last.then_inc(den_done, 1)

                def last_values(kind, b, kt):
                    if kt:
                        values(b, kt - 1, 2)
                    elif kind != "first":
                        values(b - 1, G - 1, 2)

                def step(kind, b):
                    if kind in ("pro", "tail"):
                        if kind == "tail":
                            values(b - 1, G - 1, 2)
                            denominators(b - 1, G - 1)
                        for job in SEQ[kind]:
                            fill(job, kind, b)
                            if job == "k1.1":
                                for n in range(16):
                                    scores(0, 0, n)
                                turn_max(0, 0)
                        return
                    for kt in range(4):
                        nb, nk = (b, kt + 1) if kt < 3 else (b + 1, 0)
                        more = not (kt == 3 and kind == "last")
                        for s in range(STEPS):
                            if s == TURN_AT + 1 and more:
                                turn_max(nb, nk)
                            if s == LAST_PV_AT:
                                last_values(kind, b, kt)
                            if more:
                                for n in maxima_at(kt, s)[:1]:
                                    scores(nb, nk, n)
                            for job in jobs_at(kind, kt, s):
                                fill(job, kind, b)
                            if 0 <= s - UNIT_AT < 12:
                                scores_T(b, kt, s - UNIT_AT)
                            if more:
                                for n in maxima_at(kt, s)[1:]:
                                    scores(nb, nk, n)
                            if s == LATE_AT:
                                if kt:
                                    denominators(b, kt - 1)
                                elif kind != "first":
                                    denominators(b - 1, G - 1)
                            if s in PV_AT:
                                values(b, kt, PV_AT[s])

                batches(pe, step)
        lay.close()

        tok = sb(es, "tok", [P, 2, KD, 32])
        hid = sb(es, "hid", [P, 2, BANK])
        hid_T = sb(es, "hid_T", [P, 2, HT, P])
        b1_T = sb(es, "b1_T", [P, E, HC, HT])
        b2_wide = sb(es, "b2_wide", [P, 2, D])
        o_sb = sb(es, "o_sb", [P, 2, D])
        WAYS = 4
        fin = [sb(es, f"fin{i}", [TT, 2, D]) for i in range(WAYS)]
        o_in = [sb(es, f"o_in{i}", [P, D]) for i in range(WAYS)]
        pick_now = [sb(es, f"pick_now{i}", [P, T]) for i in range(WAYS)]

        b1_flipped = sem("b1_flipped")
        b1_ready = sem("b1_ready")
        cleared = sem("cleared")
        b2_loaded = [sem(f"b2_loaded{i}") for i in range(2)]
        tok_ready = sem("tok_ready")
        h_full = sem("h_full")
        h_out = sem("h_out")
        ht_full = sem("ht_full")
        ht_biased = sem("ht_biased")
        ht_ready = sem("ht_ready")
        o_full = sem("o_full")
        o_out = sem("o_out")
        o_stored = [sem(f"o_stored{i}") for i in range(2)]
        fin_loaded = [sem(f"fin_loaded{i}") for i in range(WAYS)]
        scat_full = sem("scat_full")
        fin_ready = sem("fin_ready")
        fin_stored = [sem(f"fin_stored{i}") for i in range(WAYS)]
        NB1 = E * HC * HT // P

        def load_tokens(sp, b, slot):
            sp.dma_start(fin[slot][:], out[bass.ds(b, 1), :, :].rearrange(
                "o (t p) d -> p (o t) d", p=TT)).then_inc(fin_loaded[slot], 16)
            sp.dma_start(pick_now[slot][:], router[bass.ds(b, 1), :, :, :].rearrange(
                "o c e t -> (o c e) t")).then_inc(fin_loaded[slot], 16)

        with nc.Block() as block:
            @block.sync
            def _(sp):
                def weights(i, e2, first):
                    e = i * 2 + e2
                    for q in range(4) if not first else ():
                        slot = e2 * 4 + q
                        if q < 2:
                            sp.wait_ge(h_full, i * 2 + (e2 - 1))
                        else:
                            sp.wait_ge(o_full, i * 2 + (e2 - 1))
                        load_chunk(sp, e, q, slot)
                    if not first:
                        sp.wait_ge(o_out, i * 2 + (e2 - 1))
                    else:
                        sp.wait_ge(cleared, 2)
                    sp.dma_start(b2_wide[0:B, e2, :],
                                 w2[bass.ds(e, 1), H1, :].to_broadcast([B, D])
                                 ).then_inc(b2_loaded[e2], 16)

                weights(0, 0, True)
                weights(0, 1, True)
                with sp.Fori(1, E // 2) as i:
                    weights(i, 0, False)
                    weights(i, 1, False)
                for slot in range(WAYS):
                    load_tokens(sp, slot, slot)

            @block.gpsimd
            def _(pool):
                nc.gpsimd.memset(b2_wide[:], 0.0).then_inc(cleared, 1)
                nc.gpsimd.memset(tok[:], 0.0).then_inc(cleared, 1)

                def keep_parts(i, e2):
                    e = i * 2 + e2
                    pool.wait_ge(o_out, i * 2 + (e2 + 1))
                    for c in range(4):
                        pool.dma_start(o_parts[:, c, bass.ds(e, 1), :].rearrange(
                            "b o n -> b (o n)"), o_sb[c * 32:c * 32 + B, e2, :]
                        ).then_inc(o_stored[e2], 16)

                with pool.Fori(0, E // 2) as i:
                    keep_parts(i, 0)
                    keep_parts(i, 1)
                for e2 in range(2):
                    pool.wait_ge(o_stored[e2], 32 * E)

            @block.scalar
            def _(act):
                def hidden(i, e2, first):
                    e = i * 2 + e2
                    act.wait_ge(h_full, e + 1)
                    if not first:
                        act.wait_ge(ht_full, e - 1)
                    nc.scalar.copy(hid[:, e2, :], bank[e2][:]).then_inc(h_out, 1)
                    act.wait_ge(ht_biased, e + 1)
                    if not first:
                        act.wait_ge(o_full, e - 1)
                    nc.scalar.activation(hid_T[:, e2].rearrange("p t m -> p (t m)"),
                                         bank[2 + e2][:], ACT.Gelu).then_inc(ht_ready, 1)

                hidden(0, 0, True)
                hidden(0, 1, True)
                with act.Fori(1, E // 2) as i:
                    hidden(i, 0, False)
                    hidden(i, 1, False)

            @block.vector
            def _(dve):
                dve.wait_ge(b1_flipped, 1)
                nc.vector.tensor_copy(b1_T[:].rearrange("p e c t -> p (e c t)"), bank[4][:]
                                      ).then_inc(b1_ready, 1)
                dve.wait_ge(cleared, 2)

                def take(i, e2, first):
                    e = i * 2 + e2
                    if not first:
                        dve.wait_ge(h_full, e - 1)
                    nc.vector.tensor_copy(tok[:, e2, :, 0:B],
                                          merged_T[:, :, bass.ds(e, 1), :].rearrange(
                                              "p k o b -> p (k o) b")).then_inc(tok_ready, 1)

                def add_biases(i, e2, first):
                    e = i * 2 + e2
                    dve.wait_ge(ht_full, e + 1)
                    if first and e2 == 0:
                        dve.wait_ge(b1_ready, 1)
                    for t in range(HT):
                        ps = bank[2 + e2][:, t * P:(t + 1) * P].rearrange("p (c m) -> p c m", c=HC)
                        last = nc.vector.tensor_tensor(
                            ps, ps, b1_T[:, bass.ds(e, 1), :, t].rearrange(
                                "p o c -> p (o c)").unsqueeze(2).to_broadcast([P, HC, 32]),
                            ALU.add)
                    last.then_inc(ht_biased, 1)

                def part_out(i, e2, first):
                    e = i * 2 + e2
                    dve.wait_ge(o_full, e + 1)
                    dve.wait_ge(b2_loaded[e2], i * 16 + 16)
                    if not first:
                        dve.wait_ge(o_stored[e2], i * 64)
                    nc.vector.tensor_tensor(o_sb[:, e2, :], bank[5 + e2][:], b2_wide[:, e2, :],
                                            ALU.add).then_inc(o_out, 1)

                def pair(i, first):
                    for e2 in range(2):
                        take(i, e2, first)
                        add_biases(i, e2, first)
                        part_out(i, e2, first)

                pair(0, True)
                with dve.Fori(1, E // 2) as i:
                    pair(i, False)

            @block.tensor
            def _(pe):
                pe.wait_ge(b1_loaded, 16 * E)
                for g in range(NB1):
                    last = nc.tensor.transpose(bank[4][:, g * P:(g + 1) * P], b1_rows[:, g, :],
                                               ident[:])
                last.then_inc(b1_flipped, 1)

                def expert(i, e2, first):
                    e = i * 2 + e2
                    pe.wait_ge(tok_ready, e + 1)
                    if not first:
                        pe.wait_ge(h_out, e - 1)
                    for kd in range(KD):
                        slot = e2 * 4 + kd // 2
                        if kd % 2 == 0:
                            pe.wait_ge(chunk_in[slot], i * 16 + 16)
                        for c in range(HC):
                            col = (kd % 2) * H + c * BANK
                            last = nc.tensor.matmul(bank[e2][c * 32:(c + 1) * 32, :],
                                                    tok[:, e2, kd, :],
                                                    ring[:, slot, col:col + BANK],
                                                    start=(kd == 0), stop=(kd == KD - 1))
                    last.then_inc(h_full, 1)
                    pe.wait_ge(h_out, e + 1)
                    if not first:
                        pe.wait_ge(ht_ready, e - 1)
                    for t in range(HT):
                        last = nc.tensor.transpose(bank[2 + e2][:, t * P:(t + 1) * P],
                                                   hid[:, e2, t * P:(t + 1) * P], ident[:])
                    last.then_inc(ht_full, 1)
                    pe.wait_ge(ht_ready, e + 1)
                    if not first:
                        pe.wait_ge(o_out, e - 1)
                    for t in range(HT):
                        slot = e2 * 4 + 2 + t // 2
                        if t % 2 == 0:
                            pe.wait_ge(chunk_in[slot], (i * 16 + 16) * HC)
                        for c in range(HC):
                            col = (c * 2 + t % 2) * D
                            last = nc.tensor.matmul(bank[5 + e2][c * 32:(c + 1) * 32, :],
                                                    hid_T[:, e2, t, c * 32:(c + 1) * 32],
                                                    ring[:, slot, col:col + D],
                                                    start=(t == 0), stop=(t == HT - 1))
                    last.then_inc(o_full, 1)

                expert(0, 0, True)
                expert(0, 1, True)
                with pe.Fori(1, E // 2) as i:
                    expert(i, 0, False)
                    expert(i, 1, False)

        with nc.Block() as block:
            @block.sync
            def _(sp):
                def load(i, slot, first):
                    b = i * WAYS + slot
                    if not first:
                        sp.wait_ge(fin_stored[slot], i * 16)
                        load_tokens(sp, b, slot)
                    sp.dma_start(o_in[slot][:], o_parts[bass.ds(b, 1), :, :, :].rearrange(
                        "o c e n -> (o c e) n")).then_inc(fin_loaded[slot], 16)

                for slot in range(WAYS):
                    load(0, slot, True)
                with sp.Fori(1, B // WAYS) as i:
                    for slot in range(WAYS):
                        load(i, slot, False)

            @block.scalar
            def _(act):
                def turn(i, slot):
                    b = i * WAYS + slot
                    act.wait_ge(fin_ready, i * (2 * WAYS) + (slot * 2 + 2))
                    act.dma_start(out[bass.ds(b, 1), :, :].rearrange(
                        "o (t p) d -> p (o t) d", p=TT), fin[slot][:]
                    ).then_inc(fin_stored[slot], 16)

                with act.Fori(0, B // WAYS) as i:
                    for slot in range(WAYS):
                        turn(i, slot)
                for slot in range(WAYS):
                    act.wait_ge(fin_stored[slot], 16 * (B // WAYS))

            @block.vector
            def _(dve):
                def add(i, slot):
                    for t in range(2):
                        dve.wait_ge(scat_full, i * (2 * WAYS) + (slot * 2 + t + 1))
                        nc.vector.tensor_tensor(fin[slot][:, t, :], fin[slot][:, t, :],
                                                bank[slot * 2 + t][0:TT, :], ALU.add
                                                ).then_inc(fin_ready, 1)

                with dve.Fori(0, B // WAYS) as i:
                    for slot in range(WAYS):
                        add(i, slot)

            @block.tensor
            def _(pe):
                def scatter(i, slot, first):
                    pe.wait_ge(fin_loaded[slot], i * 48 + 48)
                    for t in range(2):
                        if not first:
                            pe.wait_ge(fin_ready, i * (2 * WAYS) + (slot * 2 + t + 1 - 2 * WAYS))
                        nc.tensor.matmul(bank[slot * 2 + t][0:TT, :],
                                         pick_now[slot][:, t * TT:(t + 1) * TT], o_in[slot][:],
                                         start=True, stop=True).then_inc(scat_full, 1)

                for slot in range(WAYS):
                    scatter(0, slot, True)
                with pe.Fori(1, B // WAYS) as i:
                    for slot in range(WAYS):
                        scatter(i, slot, False)


_INS = ["x", "ctx_512", "L0_attn_Wq", "L0_attn_Wk", "L0_attn_Wo", "L0_attn_U_b", "L0_attn_V_b",
        "L0_attn_W_b", "L0_attn_bias_b", "L0_attn_U_t", "L0_attn_V_t", "L0_attn_W_t",
        "L0_attn_X_t", "L0_attn_bias_t", "L0_attn_alpha", "L0_xattn_Wq", "L0_xattn_Wkv",
        "L0_xattn_Wo", "L0_ffn_gate_w", "L0_ffn_gate_b", "L0_ffn_w1", "L0_ffn_w2"]


def kernel(**inputs):
    import numpy as _np
    import concourse.bacc as _bacc
    from concourse.bass_utils import run_bass_kernel_spmd as _run

    nc = _bacc.Bacc("TRN2", target_bir_lowering=False, num_devices=1)
    arrays, args = {}, []
    for name in _INS:
        a = _np.ascontiguousarray(inputs[name])
        if a.ndim == 0:
            a = a.reshape(1)
        arrays[f"in_{name}"] = a
        args.append(nc.dram_tensor(f"in_{name}", a.shape, mybir.dt.from_np(a.dtype),
                                   kind="ExternalInput").ap())
    args.append(nc.dram_tensor("out_0", inputs["x"].shape, F32, kind="ExternalOutput").ap())
    build(nc, *args)
    r = _run(nc, [arrays], core_ids=[0])
    return r.results[0]["out_0"]
```
